# Optimizing a Trainium2 kernel written in Bass

```python
import numpy as np
import jax
import jax.numpy as jnp

def _softmax(x, axis=-1):
    return jax.nn.softmax(x, axis=axis)

def _gelu(x):
    return jax.nn.gelu(x, approximate=True)

def _silu(x):
    return jax.nn.silu(x)

def _sigmoid(x):
    return jax.nn.sigmoid(x)

def _layernorm(x, axis=-1, eps=1e-05):
    m = jnp.mean(x, axis=axis, keepdims=True)
    v = jnp.var(x, axis=axis, keepdims=True)
    return (x - m) / jnp.sqrt(v + eps)

def _scatter_add(tgt, idx, src, axis=0):
    return tgt.at[idx].add(src)

def _segment_sum(src, seg, n):
    return jax.ops.segment_sum(src, seg, n)
kernel_name = 'mk_xattn_ffn_d2_seqx_r4_acf1ed'

def setup_inputs(seed: int=0):
    np.random.seed(seed)
    _w = jnp.asarray

    def _rec_inputs():
        import jax
        import jax.numpy as jnp
        _rk = jax.random.key(seed)
        x = -0.0002928 + 1 * jax.random.normal(jax.random.fold_in(_rk, 1), (4, 1024, 256), jnp.float32)
        _lenS = 1024 - jax.random.randint(jax.random.fold_in(_rk, 7), (4,), 0, max(1, 1024 // 4) + 1, jnp.int32)
        _lenS2 = 77 - jax.random.randint(jax.random.fold_in(_rk, 8), (4,), 0, max(1, 77 // 4) + 1, jnp.int32)
        _ctx_1024P = jax.random.normal(jax.random.fold_in(_rk, 11), (4, 16, 256), jnp.float32)
        _ctx_1024c = jax.random.dirichlet(jax.random.fold_in(_rk, 511), 0.3 * jnp.ones((16,), jnp.float32), (4, 77))
        _ctx_1024t = jnp.einsum('bsk,bkd->bsd', _ctx_1024c, _ctx_1024P)
        _ctx_1024t = _ctx_1024t * jax.lax.rsqrt(jnp.mean(jnp.square(_ctx_1024t)) + 1e-12) * 0.953939
        ctx_1024 = -1.39393e-06 + 0.999914 * (_ctx_1024t + 0.3 * jax.random.normal(jax.random.fold_in(_rk, 611), (4, 77, 256), jnp.float32))
        return (x, ctx_1024)
    x, ctx_1024 = _rec_inputs()

    def _L0_xattn_setup():
        import jax, jax.numpy as jnp
        import numpy as np
        B, S, D_MODEL, D_K, D_V, N_HEAD = (2, 512, 256, 256, 256, 16)
        key = jax.random.key(seed)
        k1, k2, k3, k4, k5, k6, k7 = jax.random.split(key, 7)
        s = 1.0 / np.sqrt(D_MODEL)
        return {'q': jax.random.normal(k1, (B, S, D_MODEL), dtype=jnp.float32), 'k': jax.random.normal(k2, (B, S, D_MODEL), dtype=jnp.float32), 'v': jax.random.normal(k3, (B, S, D_MODEL), dtype=jnp.float32), 'Wq': jax.random.normal(k4, (D_MODEL, D_K), dtype=jnp.float32) * s, 'Wk': jax.random.normal(k5, (D_MODEL, D_K), dtype=jnp.float32) * s, 'Wv': jax.random.normal(k6, (D_MODEL, D_V), dtype=jnp.float32) * s, 'Wp': jax.random.normal(k7, (D_V, D_MODEL), dtype=jnp.float32) * (1.0 / np.sqrt(D_V))}
    _L0_xattn_all = _L0_xattn_setup()
    _L0_xattn_in = {k: v for k, v in _L0_xattn_all.items() if k in ('Wq', 'Wk', 'Wv', 'Wp')}
    del _L0_xattn_all

    def _L0_ffn_setup():
        import jax, jax.numpy as jnp
        import numpy as np
        B, S, D, H, E = (2, 512, 256, 1024, 8)
        key = jax.random.key(seed)
        k0, k1, k2, k3 = jax.random.split(key, 4)
        x = jax.random.normal(k0, (B, S, D), dtype=jnp.float32)
        router_w = jax.random.normal(k1, (E, D), dtype=jnp.float32) * 0.02
        w1 = jax.random.normal(k2, (E, D, H), dtype=jnp.float32) * 0.02
        w2 = jax.random.normal(k3, (E, H, D), dtype=jnp.float32) * 0.02
        return {'x': x, 'router_w': router_w, 'w1': w1, 'w2': w2}
    _L0_ffn_all = _L0_ffn_setup()
    _L0_ffn_in = {k: v for k, v in _L0_ffn_all.items() if k in ('router_w', 'w1', 'w2')}
    del _L0_ffn_all

    def _L1_xattn_setup():
        import jax, jax.numpy as jnp
        import numpy as np
        EMBED = 256
        HEADS = 16
        HEAD_DIM = EMBED // HEADS
        key = jax.random.key(seed)
        ks = jax.random.split(key, 8)
        N, L = (4, 512)
        inp = {'values': jax.random.normal(ks[0], (N, L, EMBED), dtype=jnp.float32), 'keys': jax.random.normal(ks[1], (N, L, EMBED), dtype=jnp.float32), 'query': jax.random.normal(ks[2], (N, L, EMBED), dtype=jnp.float32), 'Wv': jax.random.normal(ks[3], (HEAD_DIM, HEAD_DIM), dtype=jnp.float32) * (1.0 / np.sqrt(HEAD_DIM)), 'Wk': jax.random.normal(ks[4], (HEAD_DIM, HEAD_DIM), dtype=jnp.float32) * (1.0 / np.sqrt(HEAD_DIM)), 'Wq': jax.random.normal(ks[5], (HEAD_DIM, HEAD_DIM), dtype=jnp.float32) * (1.0 / np.sqrt(HEAD_DIM)), 'Wo': jax.random.normal(ks[6], (EMBED, EMBED), dtype=jnp.float32) * (1.0 / np.sqrt(EMBED)), 'bo': jax.random.normal(ks[7], (EMBED,), dtype=jnp.float32) * 0.01}
        return inp
    _L1_xattn_all = _L1_xattn_setup()
    _L1_xattn_in = {k: v for k, v in _L1_xattn_all.items() if k in ('Wv', 'Wk', 'Wq', 'Wo', 'bo')}
    del _L1_xattn_all

    def _L1_ffn_setup():
        import jax, jax.numpy as jnp
        import numpy as np
        D_MODEL, D_FF, RANK = (256, 1024, 64)
        B, S = (4, 1024)
        key = jax.random.key(seed)
        ks = jax.random.split(key, 7)
        return {'x': jax.random.normal(ks[0], (B, S, D_MODEL), dtype=jnp.float32), 'U1': jax.random.normal(ks[1], (D_MODEL, RANK), dtype=jnp.float32) * 0.02, 'V1': jax.random.normal(ks[2], (RANK, D_FF), dtype=jnp.float32) * 0.02, 'b1': jnp.zeros((D_FF,), dtype=jnp.float32), 'U2': jax.random.normal(ks[3], (D_FF, RANK), dtype=jnp.float32) * 0.02, 'V2': jax.random.normal(ks[4], (RANK, D_MODEL), dtype=jnp.float32) * 0.02, 'b2': jnp.zeros((D_MODEL,), dtype=jnp.float32)}
    _L1_ffn_all = _L1_ffn_setup()
    _L1_ffn_in = {k: v for k, v in _L1_ffn_all.items() if k in ('U1', 'V1', 'b1', 'U2', 'V2', 'b2')}
    del _L1_ffn_all
    return {'x': x, 'ctx_1024': ctx_1024, 'L0_xattn_Wq': _L0_xattn_in['Wq'], 'L0_xattn_Wk': _L0_xattn_in['Wk'], 'L0_xattn_Wv': _L0_xattn_in['Wv'], 'L0_xattn_Wp': _L0_xattn_in['Wp'], 'L0_ffn_router_w': _L0_ffn_in['router_w'], 'L0_ffn_w1': _L0_ffn_in['w1'], 'L0_ffn_w2': _L0_ffn_in['w2'], 'L1_xattn_Wv': _L1_xattn_in['Wv'], 'L1_xattn_Wk': _L1_xattn_in['Wk'], 'L1_xattn_Wq': _L1_xattn_in['Wq'], 'L1_xattn_Wo': _L1_xattn_in['Wo'], 'L1_xattn_bo': _L1_xattn_in['bo'], 'L1_ffn_U1': _L1_ffn_in['U1'], 'L1_ffn_V1': _L1_ffn_in['V1'], 'L1_ffn_b1': _L1_ffn_in['b1'], 'L1_ffn_U2': _L1_ffn_in['U2'], 'L1_ffn_V2': _L1_ffn_in['V2'], 'L1_ffn_b2': _L1_ffn_in['b2']}

def reference(x, ctx_1024, L0_xattn_Wq, L0_xattn_Wk, L0_xattn_Wv, L0_xattn_Wp, L0_ffn_router_w, L0_ffn_w1, L0_ffn_w2, L1_xattn_Wv, L1_xattn_Wk, L1_xattn_Wq, L1_xattn_Wo, L1_xattn_bo, L1_ffn_U1, L1_ffn_V1, L1_ffn_b1, L1_ffn_U2, L1_ffn_V2, L1_ffn_b2):
    import jax
    import jax.numpy as jnp

    def _L0_xattn_ref(q, k, v, Wq, Wk, Wv, Wp):
        import jax, jax.numpy as jnp
        import numpy as np
        B, S, D_MODEL, D_K, D_V, N_HEAD = (2, 512, 256, 256, 256, 16)
        b, sq, _ = q.shape
        sk = k.shape[1]
        hd_k = D_K // N_HEAD
        hd_v = D_V // N_HEAD
        Q = (q @ Wq).reshape(b, N_HEAD, sq, hd_k)
        K = (k @ Wk).reshape(b, N_HEAD, sk, hd_k)
        V = (v @ Wv).reshape(b, N_HEAD, sk, hd_v)
        wei = jnp.einsum('bhqd,bhkd->bhqk', Q, K)
        causal = jnp.arange(sq)[:, None] >= jnp.arange(sk)[None, :]
        wei = jnp.where(causal[None, None], wei, -jnp.inf)
        att = jnp.einsum('bhqk,bhkd->bhqd', jax.nn.softmax(wei, axis=-1), V)
        out = jnp.swapaxes(att, 1, 2).reshape(b, sq, D_V)
        return out @ Wp

    def _L0_ffn_ref(x, router_w, w1, w2):
        import jax, jax.numpy as jnp
        import numpy as np
        B, S, D, H, E = (2, 512, 256, 1024, 8)
        b, s, d = x.shape
        e = router_w.shape[0]
        xf = x.reshape(-1, d)
        probs = jax.nn.softmax(xf @ router_w.T, axis=-1)
        topv, topi = jax.lax.top_k(probs, 2)
        topv = topv / (topv.sum(axis=-1, keepdims=True) + 1e-09)
        cw = (jax.nn.one_hot(topi, e, dtype=xf.dtype) * topv[..., None]).sum(axis=1)
        h = jax.nn.gelu(jnp.einsum('td,edh->teh', xf, w1), approximate=False)
        y = jnp.einsum('teh,ehd->ted', h, w2)
        out = jnp.einsum('te,ted->td', cw, y)
        return out.reshape(b, s, d)

    def _L1_xattn_ref(values, keys, query, Wv, Wk, Wq, Wo, bo):
        import jax, jax.numpy as jnp
        import numpy as np
        EMBED = 256
        HEADS = 16
        HEAD_DIM = EMBED // HEADS
        N, Lq, _ = query.shape
        Lv = values.shape[1]
        Lk = keys.shape[1]
        v = values.reshape(N, Lv, HEADS, HEAD_DIM)
        k = keys.reshape(N, Lk, HEADS, HEAD_DIM)
        q = query.reshape(N, Lq, HEADS, HEAD_DIM)
        v = jnp.einsum('nlhd,ed->nlhe', v, Wv)
        k = jnp.einsum('nlhd,ed->nlhe', k, Wk)
        q = jnp.einsum('nlhd,ed->nlhe', q, Wq)
        energy = jnp.einsum('nqhd,nkhd->nhqk', q, k)
        attention = jax.nn.softmax(energy / jnp.sqrt(jnp.float32(EMBED)), axis=-1)
        out = jnp.einsum('nhql,nlhd->nqhd', attention, v).reshape(N, Lq, EMBED)
        return out @ Wo.T + bo

    def _L1_ffn_ref(x, U1, V1, b1, U2, V2, b2):
        import jax, jax.numpy as jnp
        import numpy as np
        D_MODEL, D_FF, RANK = (256, 1024, 64)
        B, S = (4, 1024)
        P = jnp.einsum('bsd,dr->bsr', x, U1)
        H = jax.nn.gelu(jnp.einsum('bsr,rf->bsf', P, V1) + b1)
        Q = jnp.einsum('bsf,fr->bsr', H, U2)
        return jnp.einsum('bsr,rd->bsd', Q, V2) + b2
    x = x + _L0_xattn_ref(_layernorm(x, axis=-1), ctx_1024, ctx_1024, L0_xattn_Wq, L0_xattn_Wk, L0_xattn_Wv, L0_xattn_Wp)
    x = x + _L0_ffn_ref(_layernorm(x, axis=-1), L0_ffn_router_w, L0_ffn_w1, L0_ffn_w2)
    x = x + _L1_xattn_ref(ctx_1024, ctx_1024, _layernorm(x, axis=-1), L1_xattn_Wv, L1_xattn_Wk, L1_xattn_Wq, L1_xattn_Wo, L1_xattn_bo)
    x = x + _L1_ffn_ref(_layernorm(x, axis=-1), L1_ffn_U1, L1_ffn_V1, L1_ffn_b1, L1_ffn_U2, L1_ffn_V2, L1_ffn_b2)
    return x

_drawn_inputs = setup_inputs


def setup_inputs(seed=0):
    import zlib

    import numpy as np

    out = dict(_drawn_inputs(seed))
    spreads = {'L1_ffn_b1': (0.0, 0.8), 'L1_ffn_b2': (0.0, 0.8)}
    factors = {'L1_xattn_bo': 7.54,
     'L1_ffn_U1': 8.0,
     'L1_ffn_V1': 8.0,
     'L1_ffn_U2': 8.0,
     'L1_ffn_V2': 8.0}
    for name, (base, spread) in spreads.items():
        noise = np.random.default_rng([zlib.crc32(name.encode()), seed]).standard_normal(out[name].shape)
        drawn = base * np.exp(spread * noise) if base else spread * noise
        out[name] = jnp.asarray(drawn.astype(out[name].dtype))
    for name, factor in factors.items():
        out[name] = (out[name] * factor).astype(out[name].dtype)
    return out
```

```python
import numpy as np
import concourse.bass as bass
from concourse import mybir
from contextlib import ExitStack

F32 = mybir.dt.float32
F16 = mybir.dt.float16
BF16 = mybir.dt.bfloat16
I32 = mybir.dt.int32
ACT = mybir.ActivationFunctionType
ALU = mybir.AluOpType
AX = mybir.AxisListType
ds = bass.ds

P = 128
B, S, D = 4, 1024, 256
KEYS = 77
HEADS = 16
HD = D // HEADS
NT = B * S // P
TB = S // P
DC = D // P
HK = HEADS * KEYS
CH = 4 * KEYS
VW = HD + 1
HR = 4 * HD
E, HID = 8, 1024
SLOTS = 256
ET = (2 * B * S + E * (SLOTS - 1)) // SLOTS
HALFT = ET * SLOTS // P
WSCALE = 64.0
MSCALE = 64.0
RANK = 64
EPS = 1e-5
NEG = -1e30

CC = {}
_at = 0
for _n, _w in (("ident", P), ("tri", P), ("rowid", P), ("halfid", HALFT), ("blocks", P // HD),
               ("rows", 3), ("early", P), ("latekeys", HEADS * KEYS), ("seen", HEADS * 5),
               ("part", 1), ("restart", E * NT), ("tileid", NT), ("rank8", E), ("slot0", ET)):
    CC[_n] = (_at, _at + _w)
    _at += _w
CW = _at


def constants():
    c = np.zeros((P, CW), np.float32)

    def put(name, v):
        a, b = CC[name]
        v = np.asarray(v, np.float32)
        c[:v.shape[0], a:b] = v.reshape(v.shape[0], b - a)

    p = np.arange(P)
    put("ident", np.eye(P))
    put("tri", p[:, None] < p[None, :])
    put("rowid", np.broadcast_to(p, (P, P)))
    put("halfid", np.broadcast_to(np.arange(HALFT), (P, HALFT)))
    put("blocks", p[:, None] // HD == np.arange(P // HD)[None, :])
    w = p % HR
    put("rows", np.stack([w < 2 * HD, (w >= 2 * HD) & (w < 3 * HD),
                          MSCALE * ((w == 3 * HD) | (w == 3 * HD + 1))], 1))
    i = np.arange(5)
    put("early", i[:, None] == p[None, :] % 64)
    j, k = np.arange(HEADS), np.arange(KEYS)
    put("latekeys", NEG * (k[None, None, :] > 16 * i[:, None, None] + j[None, :, None]))
    rj = (2 * np.arange(8)[None, :] + np.arange(2)[:, None]).reshape(-1)
    put("seen", k[:, None, None] <= 16 * i[None, None, :] + rj[None, :, None])
    put("part", p[:, None])
    put("restart", np.broadcast_to((np.arange(E * NT) % NT != 0), (P, E * NT)))
    put("tileid", np.broadcast_to(np.arange(NT), (P, NT)))
    put("rank8", np.broadcast_to(E - np.arange(E), (P, E)))
    put("slot0", np.broadcast_to(SLOTS * np.arange(ET), (P, ET)))
    return c


def flat(i, n):
    return slice(i * n, (i + 1) * n)


def after(eng, sem, value):
    if isinstance(value, int) and value <= 0:
        return
    eng.wait_ge(sem, value)


def apart(eng, sem, value, passed):
    eng.wait_ge(sem, value)
    if not isinstance(value, int):
        eng.sem_inc(passed, 1)


class Place:

    def __init__(self, nc, ctx):
        self.nc, self.ctx = nc, ctx

    def sb(self, name, shape, dt=F32):
        return self.ctx.enter_context(self.nc.sbuf_tensor(name, shape, dt))

    def bank(self, name, dt=F32):
        return self.ctx.enter_context(self.nc.psum_tensor(name, [P, 2048 // (4 if dt == F32 else 2)], dt))

    def sem(self, name):
        return self.ctx.enter_context(self.nc.semaphore(name))


def prepare(nc, A, G):
    with ExitStack() as ctx:
        L = Place(nc, ctx)
        ctx_sb = L.sb("ctx_sb", [KEYS, B, D])
        ctxT = L.sb("ctxT", [P, DC, B * KEYS])
        wk0 = L.sb("wk0", [P, DC, D])
        wv0 = L.sb("wv0", [P, DC, D])
        wk0r = L.sb("wk0r", [P, DC, HEADS, 8, HD])
        w1s = L.sb("w1s", [HD, 3, HD])
        w1r = L.sb("w1r", [HD, 4, 8, HD])
        gT = L.sb("gT", [P, P])
        gTm = L.sb("gTm", [P, 8, P])
        wvbd = L.sb("wvbd", [P, 8, HD])
        v0 = L.sb("v0", [KEYS, B, D])
        kf = L.sb("kf", [P, B * HK])
        klo = L.sb("klo", [P, HK])
        kmid = L.sb("kmid", [P, HK])
        rw = L.sb("rw", [E, D])
        wo1 = L.sb("wo1", [P, DC, D])
        bank = [L.bank(f"prep_ps{i}") for i in range(8)]
        s_in, s_const, s_w = L.sem("p_in"), L.sem("p_const"), L.sem("p_w")
        s_pe, s_act, s_dve, s_v = L.sem("p_pe"), L.sem("p_act"), L.sem("p_dve"), L.sem("p_v")
        s_k = L.sem("p_k")
        ident = G["const"][:, CC["ident"][0]:CC["ident"][1]]
        blocks = G["const"][:, CC["blocks"][0]:CC["blocks"][1]]
        rows = G["const"][:, CC["rows"][0]:CC["rows"][1]]
        steps = []
        for b in range(B):
            steps.append(("ctxT", b))
        steps += [("rwT", 0), ("woT", 0), ("woT", 1), ("gT", 0), ("wvT", 0)]
        steps += [("v0", b) for b in range(B)] + [("v1", b) for b in range(B)]
        steps += [("k0", c) for c in range(HEADS)]
        steps += [("k1", h) for h in range(HEADS)]
        index = {s: n for n, s in enumerate(steps)}
        on_act = {("k0", c) for c in range(HEADS)} | {("k1", h) for h in range(HEADS)}
        acts = [s for s in steps if s in on_act]
        dves = [s for s in steps if s not in on_act]
        with nc.Block() as block:

            @block.sync
            def _(sp):
                sp.dma_start(G["const"][:, :], A["const"]).then_inc(s_const, 16)
                sp.dma_start(ctx_sb[:, :, :], A["ctx_1024"].rearrange("b k d -> k b d")).then_inc(s_in, 16)
                sp.dma_start(wk0[:, :, :], A["L0_xattn_Wk"].rearrange("(c p) n -> p c n", p=P)).then_inc(s_in, 16)
                sp.dma_start(wv0[:, :, :], A["L0_xattn_Wv"].rearrange("(c p) n -> p c n", p=P)).then_inc(s_in, 16)
                for n, name in enumerate(("L1_xattn_Wk", "L1_xattn_Wq", "L1_xattn_Wv")):
                    sp.dma_start(w1s[:, n, :], A[name]).then_inc(s_in, 16)
                sp.dma_start(rw[:, :], A["L0_ffn_router_w"]).then_inc(s_in, 16)
                sp.dma_start(wo1[:, :, :], A["L1_xattn_Wo"].rearrange("(c p) n -> p c n", p=P)).then_inc(s_in, 16)
                sp.dma_start(G["wq0"][:, :, :], A["L0_xattn_Wq"].rearrange("(c p) n -> p c n", p=P)).then_inc(s_w, 16)
                sp.wait_ge(s_dve, dves.index(("v0", B - 1)) + 1)
                sp.dma_start(A["values0"].rearrange("b (k n) -> k b n", k=KEYS), v0[:, :, :]).then_inc(s_v, 16)
                sp.wait_ge(s_v, 16)
                for b in range(B):
                    sp.dma_start(G["v0"][:, b, :, 0:HD],
                                 A["values0"][b, :].rearrange("(h k n) -> k h n", h=HEADS, k=KEYS)).then_inc(s_v, 16)
                sp.wait_ge(s_v, 16 * (1 + B))
                sp.wait_ge(s_w, 16)

            @block.tensor
            def _(pe):
                mm = nc.tensor.matmul
                pe.wait_ge(s_const, 16)
                pe.wait_ge(s_in, 16 * 8)
                for n, (what, i) in enumerate(steps):
                    if n >= 8:
                        old = steps[n - 8]
                        if old in on_act:
                            pe.wait_ge(s_act, acts.index(old) + 1)
                        else:
                            pe.wait_ge(s_dve, dves.index(old) + 1)
                    ps = bank[n % 8]
                    if what == "ctxT":
                        for c in range(DC):
                            last = nc.tensor.transpose(ps[:, c * KEYS:(c + 1) * KEYS], ctx_sb[:, i, flat(c, P)],
                                                       ident[0:KEYS, 0:KEYS])
                    elif what == "rwT":
                        for c in range(DC):
                            last = nc.tensor.transpose(ps[:, c * E:(c + 1) * E], rw[:, flat(c, P)], ident[0:E, 0:E])
                    elif what == "woT":
                        for c in range(DC):
                            last = nc.tensor.transpose(ps[:, flat(c, P)], wo1[:, c, flat(i, P)], ident)
                    elif what == "gT":
                        pe.wait_ge(s_k, 1)
                        last = mm(ps[:, 0:P], w1r[:, 0, :, :].rearrange("p a b -> p (a b)"),
                                  w1r[:, 1, :, :].rearrange("p a b -> p (a b)"), start=True, stop=True)
                    elif what == "wvT":
                        last = mm(ps[:, 0:P], w1r[:, 2, :, :].rearrange("p a b -> p (a b)"),
                                  w1r[:, 3, :, :].rearrange("p a b -> p (a b)"), start=True, stop=True)
                    elif what == "v0":
                        pe.wait_ge(s_dve, dves.index(("ctxT", i)) + 1)
                        for c in range(DC):
                            last = mm(ps[0:KEYS, 0:D], ctxT[:, c, flat(i, KEYS)], wv0[:, c, :],
                                      start=c == 0, stop=c == DC - 1)
                    elif what == "v1":
                        pe.wait_ge(s_dve, dves.index(("wvT", 0)) + 1)
                        for c in range(DC):
                            last = mm(ps[0:KEYS, flat(c, P)], ctxT[:, c, flat(i, KEYS)],
                                      wvbd[:, :, :].rearrange("p a b -> p (a b)"), start=True, stop=True)
                    elif what == "k0":
                        for c in range(DC):
                            last = mm(ps[:, 0:B * KEYS], wk0r[:, c, i, :, :].rearrange("p a b -> p (a b)"),
                                      ctxT[:, c, :], start=c == 0, stop=c == DC - 1)
                    elif what == "k1":
                        last = mm(ps[:, 0:B * KEYS], gTm[:, i % 8, :], ctxT[:, i // 8, :], start=True, stop=True)
                    last.then_inc(s_pe, 1)

            @block.scalar
            def _(act):
                for m, (what, i) in enumerate(acts):
                    act.wait_ge(s_pe, index[(what, i)] + 1)
                    src = bank[index[(what, i)] % 8][:, 0:B * KEYS].rearrange("p (b k) -> p b k", b=B)
                    if what == "k0":
                        dst = kf[:, :].rearrange("p (b k c) -> p b k c", b=B, c=HEADS)[:, :, :, i]
                    else:
                        if i == 0:
                            act.wait_ge(s_k, 1 + 3 * B)
                        dst = kf[:, :].rearrange("p (b h k) -> p b h k", b=B, h=HEADS)[:, :, i, :]
                    nc.scalar.activation(dst, src, ACT.Copy).then_inc(s_act, 1)

            @block.vector
            def _(dve):
                dve.wait_ge(s_in, 16 * 8)
                dve.wait_ge(s_const, 16)
                for n in range(3):
                    nc.vector.tensor_copy(w1r[:, n, :, :], w1s[:, n, :][:, None, :].broadcast_to([HD, 8, HD]))
                nc.vector.tensor_copy(w1r[:, 3, :, :], ident[0:HD, 0:HD][:, None, :].broadcast_to([HD, 8, HD]))
                for c in range(DC):
                    last = nc.vector.tensor_copy(
                        wk0r[:, c, :, :, :],
                        wk0[:, c, :].rearrange("p (h e) -> p h e", h=HEADS)[:, :, None, :].broadcast_to([P, HEADS, 8, HD]))
                last.then_inc(s_k, 1)
                nc.vector.memset(G["v0"][:, :, :, HD:VW], 1.0)
                nc.vector.memset(G["v1"][:, :, :, HD:VW], 1.0)
                nc.vector.tensor_copy(G["ident16"][:, :], ident)
                nc.vector.tensor_copy(G["tri16"][:, :], G["const"][:, CC["tri"][0]:CC["tri"][1]])
                nc.vector.memset(G["ones16"][:, :], 1.0)
                nc.vector.tensor_copy(G["early"][:, :], G["const"][0:5, CC["early"][0]:CC["early"][1]])
                nc.vector.tensor_copy(G["late"][:, :], G["const"][0:5, CC["latekeys"][0]:CC["latekeys"][1]])
                nc.vector.tensor_copy(G["blocks16"][:, :], blocks)
                nc.vector.memset(G["neghalf"][:, :], -0.5)
                for what, i in dves:
                    dve.wait_ge(s_pe, index[(what, i)] + 1)
                    ps = bank[index[(what, i)] % 8]
                    if what == "ctxT":
                        last = nc.vector.tensor_copy(ctxT[:, :, flat(i, KEYS)],
                                                     ps[:, 0:DC * KEYS].rearrange("p (c k) -> p c k", c=DC))
                    elif what == "rwT":
                        last = nc.vector.tensor_copy(G["rwT"][:, :, :], ps[:, 0:DC * E].rearrange("p (c k) -> p c k", c=DC))
                    elif what == "woT":
                        last = nc.vector.tensor_copy(G["woT"][:, i, :], ps[:, 0:D])
                    elif what == "gT":
                        for m in range(8):
                            last = nc.vector.tensor_scalar(gTm[:, m, :], ps[:, 0:P], blocks[:, m:m + 1], None, ALU.mult)
                    elif what == "wvT":
                        last = nc.vector.tensor_tensor(wvbd[:, :, :], ps[:, 0:P].rearrange("p (a b) -> p a b", a=8),
                                                       blocks[:, :, None].broadcast_to([P, 8, HD]), ALU.mult)
                    elif what == "v0":
                        last = nc.vector.tensor_copy(v0[:, i, :], ps[0:KEYS, 0:D])
                    elif what == "v1":
                        last = nc.vector.tensor_copy(G["v1"][:, i, :, 0:HD],
                                                     ps[0:KEYS, 0:D].rearrange("p (h e) -> p h e", h=HEADS))
                    last.then_inc(s_dve, 1)
                for layer in range(2):
                    dve.wait_ge(s_act, HEADS * (layer + 1))
                    for b in range(B):
                        k = 1 + 3 * (B * layer + b)
                        hi = G["khi"][layer][:, b, :]
                        src = kf[:, flat(b, HK)]
                        nc.vector.tensor_copy(hi, src).then_inc(s_k, 1)
                        dve.wait_ge(s_k, k + 1)
                        nc.vector.tensor_tensor(klo[:, :], src, hi, ALU.subtract).then_inc(s_k, 1)
                        dve.wait_ge(s_k, k + 2)
                        nc.vector.tensor_scalar(kmid[:, :], klo[:, :], rows[:, 1:2], rows[:, 2:3], ALU.mult, ALU.add) \
                            .then_inc(s_k, 1)
                        dve.wait_ge(s_k, k + 3)
                        nc.vector.scalar_tensor_tensor(G["kcat"][layer][:, b, :], hi, rows[:, 0:1], kmid[:, :],
                                                       ALU.mult, ALU.add)


def attention(nc, A, G, layer):
    first = layer == 0
    with ExitStack() as ctx:
        L = Place(nc, ctx)
        x = L.sb(f"x{layer}", [P, 4, D])
        stats = L.sb(f"stats{layer}", [P, 4, 6])
        mv = L.sb(f"mv{layer}", [P, 4, 2])
        ve = L.sb(f"ve{layer}", [P, 4, 1])
        rstd = L.sb(f"rstd{layer}", [P, 4, 1])
        xh = L.sb(f"xh{layer}", [P, 4, D])
        xhT = L.sb(f"xhT{layer}", [P, 2, D])
        qcat = L.sb(f"qcat{layer}", [P, 4, HEADS, HR], F16)
        qhi = L.sb(f"qhi{layer}", [P, 4, D], F16)
        qhT = L.sb(f"qhT{layer}", [P, 2, DC, P], F16)
        nmax = L.sb(f"nmax{layer}", [P, 2, HEADS])
        bd = L.sb(f"bd{layer}", [P, 2, 2, 8, KEYS], F16)
        kcat = L.sb(f"kcat_u{layer}", [P, 2, HK], F16)
        vu = L.sb(f"vu{layer}", [KEYS, 2, HEADS, VW])
        qT = L.sb(f"qT{layer}", [P, 2, 8, P], F16)
        pT = L.sb(f"pT{layer}", [KEYS, 2, 8 * S])
        rec = L.sb(f"rec{layer}", [P, 2, HEADS])
        o = L.sb(f"o{layer}", [P, 2, HEADS, HD])
        y1 = y2 = None
        if not first:
            y1 = L.sb("y1", [P, 4, D])
            y2 = L.sb("y2", [P, 4, D])
            xa = L.sb("xa", [P, 2, D])
            x2 = L.sb("x2", [P, 4, D])
            slots = L.sb("slots", [P, 4, 2], I32)
        tr_ps = L.bank(f"tr_ps{layer}")
        qh_ps = tr_ps[:, 0:P].bitcast(F16)
        q_ps = L.bank(f"q_ps{layer}")
        s_ps = [L.bank(f"s_ps{layer}_{i}") for i in range(2)]
        qT_ps = L.bank(f"qT_ps{layer}", F16)
        sT_ps = [L.bank(f"sT_ps{layer}_{i}") for i in range(2)]
        o_ps = L.bank(f"o_ps{layer}")
        sem = lambda n: L.sem(f"{n}_{layer}")
        x_in = [sem(f"x_in{i}") for i in range(4)]
        y_in = [sem(f"y_in{i}") for i in range(4)] if not first else None
        var_ok, rstd_ok, xh_ok, norm_ch = sem("var_ok"), sem("rstd_ok"), sem("xh_ok"), sem("norm_ch")
        qhi_ok, qlo_ok = sem("qhi_ok"), sem("qlo_ok")
        if first:
            xhT_ps, xhT_ok, q_done, mask_ok = (sem(n) for n in ("xhT_ps", "xhT_ok", "q_done", "mask_ok"))
        qhT_ps, qhT_ok, bd_ok, s_done, max_ok, m_ok, m_ch = (
            sem(n) for n in ("qhT_ps", "qhT_ok", "bd_ok", "s_done", "max_ok", "m_ok", "m_ch"))
        kcat_ok, vu_ok, qT_done, qT_ok, sT_done, exp_ok = (
            sem(n) for n in ("kcat_ok", "vu_ok", "qT_done", "qT_ok", "sT_done", "exp_ok"))
        o_done, rec_ok, o_ok = sem("o_done"), sem("rec_ok"), sem("o_ok")
        o_out = [sem(f"o_out{i}") for i in range(2)]
        if not first:
            slots_ok, x2_ok, x2_out = sem("slots_ok"), sem("x2_ok"), [sem(f"x2_out{i}") for i in range(4)]
        ident = G["const"][:, CC["ident"][0]:CC["ident"][1]]
        seen = G["const"][0:KEYS, CC["seen"][0]:CC["seen"][1]].rearrange("p (c t) -> p c t", t=5)
        OUTS = 4 if first else 1
        AHEAD = 16

        def batches(eng, step, ahead=False):
            def body(bb, lo, hi, end):
                for s in range(TB):
                    step(bb, s, lambda k: lo <= s - k < (hi if k >= 0 else end))
            body(0, 0, TB, TB + 1)
            with eng.Fori(1, B - 1 if ahead else B) as bb:
                body(bb, -TB, TB, TB + 1)
            if ahead:
                body(B - 1, -TB, TB, TB)
            body(B, -TB, 0, 0)

        def count(bb, s, back, per=1, plus=0):
            return bb * (TB * per) + ((s - back) * per + plus)

        def times4(bb, s, back, per=16):
            return bb * (2 * per) + ((s - back) // 4 + 1) * per

        def times2(bb, s, back, per):
            return bb * (4 * per) + ((s - back) // 2 + 1) * per

        src_x = A["x"].rearrange("b s d -> (b s) d") if first else A["x1"]
        with nc.Block() as block:

            @block.sync
            def _(sp):
                for k in range(2):
                    sp.sem_inc(o_out[k], AHEAD)

                def load(bb, s):
                    after(sp, xh_ok if first else x2_ok, count(bb, s, 4, 1, 1))
                    sp.dma_start(x[:, s % 4, :], src_x[ds(bb * S + s * P, P), :]).then_inc(x_in[s % 4], 16)

                load(0, 0)

                def step(bb, s, live):
                    if live(-1):
                        load(bb, s + 1)
                    if not first and live(2):
                        k = (s - 2) % 4
                        sp.wait_ge(x2_ok, count(bb, s, 2, 1, 1))
                        sp.dma_start(A["x2"][ds(bb * S + (s - 2) * P, P), :], x2[:, k, :]).then_inc(x2_out[k], 16)
                    if live(8):
                        k, u = s % 2, s // 4
                        sp.wait_ge(o_ok, count(bb, s, 8, 1, 1) + AHEAD)
                        if first:
                            for n in range(2):
                                st = 2 * (s % 4) + n
                                r, q = st // 4, st % 4
                                for jp in range(2):
                                    dst = A["attn"].rearrange("(b t q j r) d -> b q j r t d", b=B, q=4, j=2, r=2)
                                    sp.dma_start(dst[ds(bb - 1, 1), q, jp, r, :, flat(u, P)],
                                                 o[flat(jp, 64), k, flat(n, 8), :].rearrange("p h e -> p (h e)")) \
                                        .then_inc(o_out[k], 16)
                        else:
                            sp.dma_start(A["attn1"][ds(bb * S + (s - 8) * P, P), :],
                                         o[:, k, :, :].rearrange("p h e -> p (h e)")).then_inc(o_out[k], 16)
                batches(sp, step, ahead=True)
                for k in range(2):
                    sp.wait_ge(o_out[k], 16 * OUTS * NT // 2 + AHEAD)
                if not first:
                    for k in range(4):
                        sp.wait_ge(x2_out[k], 16 * NT // 4)

            @block.gpsimd
            def _(pool):
                def gather(bb, s):
                        after(pool, x2_ok, count(bb, s, 4, 1, 1))
                        bs, ss = (bb, s) if s < TB else (bb + 1, s - TB)
                        nc.gpsimd.tensor_copy(slots[:, s % 4, :], G["slots_t"][:, ss, :, ds(bs, 1)]).then_inc(slots_ok, 1)
                        apart(pool, slots_ok, count(bb, s, 0, 1, 1), G["pool_passed"])
                        for n, y in enumerate((y1, y2)):
                            pool.indirect_dma_start(
                                out=y[:, s % 4, :], out_offset=None, in_=A["y"],
                                in_offset=bass.IndirectOffsetOnAxis(ap=slots[:, s % 4, n:n + 1], axis=0)) \
                                .then_inc(y_in[s % 4], 16)

                if not first:
                    gather(0, 0)

                def step(bb, s, live):
                    h = s // 4
                    if not first and live(-1):
                        gather(bb, s + 1)
                    if first and live(2) or not first and live(0) and s % 4 == 0:
                        k = s - 2 if first else s
                        u = k // 4
                        ring = k % 2 if first else h
                        for n in range(2):
                            if first:
                                base = bb * HK + ((2 * k + n) * KEYS if k >= 0 else (2 * (k + TB) + n) * KEYS - HK)
                                if n == 0 and live(4):
                                    apart(pool, s_done, count(bb, s, 4, 4, 4), G["pool_passed"])
                                src = G["khi"][0][:, :, :].rearrange("p b f -> p (b f)")[:, None, ds(base, KEYS)] \
                                    .broadcast_to([P, 8, KEYS])
                            else:
                                if n == 0 and live(5):
                                    apart(pool, s_done, count(bb, s, 5, 4, 4), G["pool_passed"])
                                src = G["khi"][1][:, :, :].rearrange("p b f -> p (b f)")[
                                    :, ds(bb * HK + n * 8 * KEYS, 8 * KEYS)].rearrange("p (j k) -> p j k", j=8)
                            nc.gpsimd.tensor_tensor(bd[:, ring, n, :, :], src,
                                                    G["blocks16"][:, :, None].broadcast_to([P, 8, KEYS]), ALU.mult) \
                                .then_inc(bd_ok, 1)
                    if live(0):
                        pool.wait_ge(var_ok, count(bb, s, 0, 1, 1))
                        nc.gpsimd.tensor_tensor(rstd[:, s % 4, :], ve[:, s % 4, :], G["neghalf"][:, :], ALU.pow) \
                            .then_inc(rstd_ok, 1)
                batches(pool, step, ahead=not first)

            @block.tensor
            def _(pe):
                mm = nc.tensor.matmul
                pe.sem_inc(o_done, AHEAD)

                def high_transposed(bb, s, live):
                    k = (s - 2) % 4
                    pe.wait_ge(qhi_ok, count(bb, s, 2, 1, 1))
                    if first:
                        pe.wait_ge(xhT_ok, count(bb, s, 1, 1, 1 if live(1) else 0))
                    else:
                        after(pe, qhT_ok, count(bb, s, 3, 1, 1))
                    for c in range(DC):
                        last = nc.tensor.transpose(qh_ps[:, flat(c, P)], qhi[:, k, flat(c, P)], G["ident16"][:, :])
                    last.then_inc(qhT_ps, 1)

                def queries(bb, s):
                    k = (s - 1) % 2
                    pe.wait_ge(xhT_ok, count(bb, s, 1, 1, 1))
                    after(pe, qlo_ok, count(bb, s, 2, 1, 1))
                    for c in range(DC):
                        last = mm(q_ps[:, 0:D], xhT[:, k, flat(c, P)], G["wq0"][:, c, :], start=c == 0, stop=c == DC - 1)
                    last.then_inc(q_done, 1)

                def rows_transposed(bb, s, live):
                    pe.wait_ge(xh_ok, count(bb, s, 0, 1, 1))
                    if live(2):
                        pe.wait_ge(qhT_ok, count(bb, s, 2, 1, 1))
                    else:
                        after(pe, xhT_ok, count(bb, s, 1, 1, 1))
                    for c in range(DC):
                        last = nc.tensor.transpose(tr_ps[:, flat(c, P)], xh[:, s % 4, flat(c, P)], ident)
                    last.then_inc(xhT_ps, 1)

                def scores(bb, s, g):
                    k = (s - 2) % 2
                    if g == 0:
                        pe.wait_ge(qhT_ok, count(bb, s, 2, 1, 1))
                        if first:
                            pe.wait_ge(bd_ok, count(bb, s, 2, 2, 2))
                        else:
                            pe.wait_ge(bd_ok, bb * 4 + ((s - 2) // 4 + 1) * 2)
                    ps = s_ps[g % 2][:, 0:CH]
                    after(pe, max_ok, count(bb, s, 2, 4, g - 1))
                    cols = slice(g % 2 * 4, g % 2 * 4 + 4)
                    if first:
                        for n in range(2):
                            mm(ps[flat(n, 64), :], qhT[:, k, g // 2, flat(n, 64)],
                               bd[:, k, n, cols, :].rearrange("p j k -> p (j k)"), start=True, stop=False)
                        last = mm(ps, G["early"][:, :], G["late"][:, flat(g, CH)], start=False, stop=True)
                    else:
                        last = mm(ps, qhT[:, k, g // 2, :],
                                  bd[:, (s - 2) % TB // 4, g // 2, cols, :].rearrange("p j k -> p (j k)"),
                                  start=True, stop=True)
                    last.then_inc(s_done, 1)

                def all_transposed(bb, s):
                    k = (s - 3) % 4
                    pe.wait_ge(m_ok, count(bb, s, 3, 1, 1))
                    pe.wait_ge(qlo_ok, count(bb, s, 3, 1, 1))
                    after(pe, qT_ok, count(bb, s, 4, 1, 1))
                    for j in range(8):
                        last = nc.tensor.transpose(qT_ps[:, flat(j, P)],
                                                   qcat[:, k, 2 * j:2 * j + 2, :].rearrange("p a b -> p (a b)"),
                                                   G["ident16"][:, :])
                    last.then_inc(qT_done, 1)

                def scores_by_key(bb, s, g):
                    k, h = (s - 4) % TB, (s - 4) % TB // 4
                    if g == 0:
                        pe.wait_ge(qT_ok, count(bb, s, 4, 1, 1))
                        pe.wait_ge(kcat_ok, bb * 2 + ((s - 4) // 4 + 1))
                    ps = sT_ps[g % 2][0:KEYS, :]
                    after(pe, exp_ok, count(bb, s, 4, 4, g - 1))
                    r = g % 2
                    if first:
                        n = g // 2
                        last = mm(ps, kcat[flat(r, HR), h, flat(2 * k + n, KEYS)],
                                  qT[flat(r, HR), k % 2, :, flat(n, 64)], start=True, stop=True)
                    else:
                        for i in range(4):
                            jj = g // 2 * 4 + i
                            last = mm(ps[:, flat(i, P)], kcat[flat(r, HR), h, flat(2 * jj + r, KEYS)],
                                      qT[flat(r, HR), k % 2, jj, :], start=True, stop=True)
                    last.then_inc(sT_done, 1)

                def values(bb, s, part):
                    u = s // 4
                    if part == 0:
                        pe.wait_ge(vu_ok, bb * 2 + u - 1)
                        if first:
                            pe.wait_ge(mask_ok, bb * TB + (u * 4 - 4))
                        else:
                            pe.wait_ge(exp_ok, count(bb, s, 8, 4, 4))
                        pe.wait_ge(o_ok, count(bb, s, 9, 1, 1) + AHEAD)
                    for m in range(part * 4, part * 4 + 4):
                        n, hl = m // 8, m % 8
                        if first:
                            st = 2 * (s % 4) + n
                            probs = pT[:, u, ds(hl * S + st * P, P)]
                            vals = vu[:, u, u * 8 + hl, :]
                        else:
                            place = m // 8 * 8 + m % 2 * 4 + m // 2 % 4
                            probs = pT[:, u, ds(s % 4 * (HEADS * P) + place * P, P)]
                            vals = vu[:, u, m, :]
                        last = mm(o_ps[:, ds(m * VW, VW)], probs, vals, start=True, stop=True)
                    if part == 3:
                        last.then_inc(o_done, 1)

                def step(bb, s, live):
                    if live(2):
                        high_transposed(bb, s, live)
                    if live(4):
                        scores_by_key(bb, s, 0)
                        scores_by_key(bb, s, 1)
                    if live(3):
                        all_transposed(bb, s)
                    if first and live(1):
                        queries(bb, s)
                    for g in range(4):
                        if live(2):
                            scores(bb, s, g)
                        if live(4) and g in (1, 2):
                            scores_by_key(bb, s, g + 1)
                        if live(8):
                            values(bb, s, g)
                    if first and live(0):
                        rows_transposed(bb, s, live)
                batches(pe, step)

            @block.scalar
            def _(act):
                def exps(bb, s, g):
                    k, h = (s - 4) % TB, (s - 4) % TB // 4
                    if g == 0 and not (isinstance(bb, int) and bb * TB + s < 12):
                        act.wait_ge(o_done, bb * TB + ((s - 4) // 4 * 4 - 4) + AHEAD)
                    act.wait_ge(sT_done, count(bb, s, 4, 4, g + 1))
                    if first:
                        n, r = g // 2, g % 2
                        dst = pT[:, h, ds((2 * (k % 4) + n) * S + r * 512, 512)]
                    else:
                        dst = pT[:, h, ds(k % 4 * (HEADS * P) + g * 512, 512)]
                    nc.scalar.activation(dst, sT_ps[g % 2][0:KEYS, :], ACT.Exp,
                                         scale=1.0 if first else 1.0 / 16).then_inc(exp_ok, 1)

                def step(bb, s, live):
                    if live(4):
                        exps(bb, s, 0)
                        exps(bb, s, 1)
                    if live(1):
                        k = (s - 1) % 4
                        if first:
                            act.wait_ge(q_done, count(bb, s, 1, 1, 1))
                            src = q_ps[:, 0:D]
                        else:
                            act.wait_ge(xh_ok, count(bb, s, 1, 1, 1))
                            src = xh[:, k, :]
                        after(act, qT_done, count(bb, s, 5, 1, 1))
                        nc.scalar.activation(qhi[:, k, :], src, ACT.Copy).then_inc(qhi_ok, 1)
                    if live(3):
                        k = (s - 3) % 2
                        act.wait_ge(qT_done, count(bb, s, 3, 1, 1))
                        after(act, sT_done, count(bb, s, 5, 4, 4))
                        nc.scalar.activation(qT[:, k, :, :], qT_ps[:, :].rearrange("p (j t) -> p j t", j=8),
                                             ACT.Copy).then_inc(qT_ok, 1)
                    if live(4):
                        exps(bb, s, 2)
                        exps(bb, s, 3)
                    if first and live(0):
                        act.wait_ge(xhT_ps, count(bb, s, 0, 1, 1))
                        after(act, q_done, count(bb, s, 2, 1, 1))
                        nc.scalar.activation(xhT[:, s % 2, :], tr_ps[:, 0:D], ACT.Copy).then_inc(xhT_ok, 1)
                batches(act, step)

            @block.vector
            def _(dve):
                nc.vector.memset(qcat[:, :, :, :], 0.0)
                dve.sem_inc(o_ok, AHEAD)

                def residual(bb, s):
                    k = s % 4
                    dve.wait_ge(y_in[k], times4(bb, s, 0, 32))
                    dve.wait_ge(x_in[k], times4(bb, s, 0, 16))
                    after(dve, x2_out[k], times4(bb, s, 4, 16))
                    nc.vector.scalar_tensor_tensor(xa[:, s % 2, :], y1[:, k, :], G["cw_t"][:, s, 0, ds(bb, 1)],
                                                   x[:, k, :], ALU.mult, ALU.add).then_inc(norm_ch, 1)
                    dve.wait_ge(norm_ch, count(bb, s, 0, 3, 1))
                    nc.vector.scalar_tensor_tensor(x2[:, k, :], y2[:, k, :], G["cw_t"][:, s, 1, ds(bb, 1)],
                                                   xa[:, s % 2, :], ALU.mult, ALU.add).then_inc(x2_ok, 1)
                    dve.wait_ge(x2_ok, count(bb, s, 0, 1, 1))

                def maximum(bb, s, g):
                    dve.wait_ge(s_done, count(bb, s, 2, 4, g + 1))
                    nc.vector.tensor_reduce(nmax[:, s % 2, 4 * g:4 * g + 4],
                                            s_ps[g % 2][:, 0:CH].rearrange("p (j k) -> p j k", j=4),
                                            AX.X, ALU.max, negate=True).then_inc(max_ok, 1)

                def step(bb, s, live):
                    if s % 4 == 0 and live(0):
                        after(dve, sT_done, count(bb, s, 4, 4, 0))
                        n0, n1 = ((s // 4) * 8 * KEYS, 8 * KEYS) if first else (0, HK)
                        nc.vector.tensor_scalar(kcat[:, s // 4, ds(n0, n1)],
                                                G["kcat"][layer][:, :, :].rearrange("p b f -> p (b f)")[:, ds(bb * HK + n0, n1)],
                                                1.0, None, ALU.mult) \
                            .then_inc(kcat_ok, 1)
                    if live(2):
                        dve.wait_ge(qhT_ps, count(bb, s, 2, 1, 1))
                        after(dve, s_done, count(bb, s, 4, 4, 4))
                        nc.vector.tensor_copy(qhT[:, (s - 2) % 2, :, :], qh_ps[:, 0:D].rearrange("p (c t) -> p c t", c=DC)) \
                            .then_inc(qhT_ok, 1)
                    if live(0):
                        k = s % 4
                        if first:
                            dve.wait_ge(x_in[k], times4(bb, s, 0, 16))
                            xin, per = x, 2
                        else:
                            residual(bb, s)
                            xin, per = x2, 3
                        nc.vector.bn_stats(stats[:, k, :], xin[:, k, :]).then_inc(norm_ch, 1)
                        apart(dve, norm_ch, count(bb, s, 0, per, per - 1), G["dve_passed"])
                        nc.vector.bn_aggr(mv[:, k, :], stats[:, k, :]).then_inc(norm_ch, 1)
                        dve.wait_ge(norm_ch, count(bb, s, 0, per, per))
                        nc.vector.tensor_scalar(ve[:, k, :], mv[:, k, 1:2], EPS, None, ALU.add).then_inc(var_ok, 1)
                    if live(2):
                        maximum(bb, s, 0)
                    if live(1):
                        k = (s - 1) % 4
                        src = q_ps[:, 0:D] if first else xh[:, k, :]
                        dve.wait_ge(qhi_ok, count(bb, s, 1, 1, 1))
                        hi = qhi[:, k, :].rearrange("p (h e) -> p h e", h=HEADS)
                        nc.vector.tensor_copy(qcat[:, k, :, 0:HD], hi)
                        nc.vector.tensor_copy(qcat[:, k, :, 2 * HD:3 * HD], hi)
                        nc.vector.tensor_tensor(qcat[:, k, :, HD:2 * HD], src.rearrange("p (h e) -> p h e", h=HEADS),
                                                hi, ALU.subtract).then_inc(qlo_ok, 1)
                    if live(2):
                        maximum(bb, s, 1)
                    if live(0):
                        k = s % 4
                        dve.wait_ge(rstd_ok, count(bb, s, 0, 1, 1))
                        if first:
                            after(dve, xhT_ps, count(bb, s, 4, 1, 1))
                        else:
                            after(dve, qlo_ok, count(bb, s, 4, 1, 1))
                        nc.vector.tensor_scalar(xh[:, k, :], (x if first else x2)[:, k, :], mv[:, k, 0:1],
                                                rstd[:, k, :], ALU.subtract, ALU.mult).then_inc(xh_ok, 1)
                    if live(2):
                        maximum(bb, s, 2)
                        maximum(bb, s, 3)
                        q4 = qcat[:, (s - 2) % 4, :, :]
                        dve.wait_ge(max_ok, count(bb, s, 2, 4, 4))
                        nc.vector.tensor_scalar(q4[:, :, 3 * HD], nmax[:, s % 2, :], 1 / MSCALE, None, ALU.mult).then_inc(m_ch, 1)
                        dve.wait_ge(m_ch, count(bb, s, 2, 1, 1))
                        nc.vector.scalar_tensor_tensor(q4[:, :, 3 * HD + 1], nmax[:, s % 2, :], 1 / MSCALE, q4[:, :, 3 * HD],
                                                       ALU.mult, ALU.subtract).then_inc(m_ok, 1)
                    if first and live(4):
                        k, h = (s - 4) % TB, (s - 4) % TB // 4
                        for n in range(2):
                            dve.wait_ge(exp_ok, count(bb, s, 4, 4, 2 * n + 2))
                            part = pT[:, h, ds((2 * (k % 4) + n) * S, S)].rearrange("p (c t) -> p c t", t=64)[:, :, 0:5]
                            last = nc.vector.scalar_tensor_tensor(part, part, 3e38, seen, ALU.min, ALU.mult)
                        last.then_inc(mask_ok, 1)
                    if live(8):
                        dve.wait_ge(o_done, count(bb, s, 8, 1, 1) + AHEAD)
                        k = s % 2
                        ov = o_ps[:, 0:HEADS * VW].rearrange("p (h e) -> p h e", h=HEADS)
                        if not (isinstance(bb, int) and bb * TB + s < 10):
                            dve.wait_ge(o_out[k], times2(bb, s, 10, 16 * OUTS) + AHEAD)
                        nc.vector.reciprocal(rec[:, k, :], ov[:, :, HD]).then_inc(rec_ok, 1)
                        dve.wait_ge(rec_ok, count(bb, s, 8, 1, 1))
                        nc.vector.tensor_tensor(o[:, k, :, :], ov[:, :, 0:HD],
                                                rec[:, k, :, None].broadcast_to([P, HEADS, HD]), ALU.mult).then_inc(o_ok, 1)
                    if s % 4 == 3 and live(7):
                        if not (isinstance(bb, int) and bb * TB + s < 11):
                            dve.wait_ge(o_done, bb * TB + (s - 11) + AHEAD)
                        src = G["v0"] if first else G["v1"]
                        nc.vector.tensor_scalar(vu[:, (s - 7) % TB // 4, :, :],
                                                src[:, ds(bb if s >= 7 else bb - 1, 1), :, :].rearrange("p o h e -> p (o h) e"),
                                                1.0, None, ALU.mult).then_inc(vu_ok, 1)
                batches(dve, step)


def allocate(nc, ctx):
    L = Place(nc, ctx)
    return {
        "dve_passed": L.sem("dve_passed"), "pool_passed": L.sem("pool_passed"),
        "const": L.sb("const", [P, CW]), "ident16": L.sb("ident16", [P, P], F16), "tri16": L.sb("tri16", [P, P], F16),
        "ones16": L.sb("ones16", [P, P], F16), "blocks16": L.sb("blocks16", [P, 8], F16),
        "neghalf": L.sb("neghalf", [P, 1]), "rwT": L.sb("rwT", [P, DC, E]),
        "woT": L.sb("woT", [P, DC, D]),
        "v1": L.sb("v1_sb", [KEYS, B, HEADS, VW]),
        "logits": L.sb("logits", [P, NT, E]), "cw_t": L.sb("cw_t", [P, TB, 2, B]),
        "slots_t": L.sb("slots_t", [P, TB, 2, B], I32), "token": L.sb("token", [P, HALFT], I32),
        "tile_expert": L.sb("tile_expert", [1, ET], I32),
        "khi": [None, L.sb("khi1", [P, B, HK], F16)], "kcat": [None, L.sb("kcat1", [P, B, HK], F16)],
    }


def allocate_first(nc, ctx, G):
    L = Place(nc, ctx)
    G["early"], G["late"] = L.sb("early", [5, P], BF16), L.sb("late", [5, HEADS * KEYS], BF16)
    G["wq0"], G["v0"] = L.sb("wq0", [P, DC, D]), L.sb("v0_sb", [KEYS, B, HEADS, VW])
    G["khi"][0], G["kcat"][0] = L.sb("khi0", [P, B, HK], F16), L.sb("kcat0", [P, B, HK], F16)


def normed(nc, dve, xin, stats, mv, ve, sem, at, var_ok, passed):
    nc.vector.bn_stats(stats, xin).then_inc(sem, 1)
    apart(dve, sem, at + 1, passed)
    nc.vector.bn_aggr(mv, stats).then_inc(sem, 1)
    dve.wait_ge(sem, at + 2)
    nc.vector.tensor_scalar(ve, mv[:, 1:2], EPS, None, ALU.add).then_inc(var_ok, 1)


def project(nc, A, G):
    RING = 4
    with ExitStack() as ctx:
        L = Place(nc, ctx)
        at = L.sb("at_p", [P, RING, D])
        x = L.sb("x_p", [P, RING, D])
        w = L.sb("w_p", [P, RING, HID])
        atT = L.sb("atT_p", [P, 2, D])
        x1 = L.sb("x1_p", [P, RING, D])
        xh = L.sb("xh_p", [P, RING, D])
        xhT = L.sb("xhT_p", [P, 2, D])
        wp = L.sb("wp", [P, DC, D])
        stats, mv = L.sb("stats_p", [P, RING, 6]), L.sb("mv_p", [P, RING, 2])
        ve, rstd = L.sb("ve_p", [P, RING, 1]), L.sb("rstd_p", [P, RING, 1])
        at_ps, pr_ps, xh_ps, lg_ps = (L.bank(f"{n}_ps_p") for n in ("at", "pr", "xh", "lg"))
        s_wp = L.sem("wp_in")
        ax_in = [L.sem(f"ax_in{i}") for i in range(RING)]
        w_in = [L.sem(f"w_in{i}") for i in range(RING)]
        x1_out = [L.sem(f"x1_out{i}") for i in range(RING)]
        at_done, atT_ok, pr_done, x1_ok, ch, var_ok, rstd_ok, xh_ok = (
            L.sem(f"{n}_p") for n in ("at_done", "atT_ok", "pr_done", "x1_ok", "ch", "var_ok", "rstd_ok", "xh_ok"))
        xh_done, xhT_ok, lg_done, lg_ok, whi_ok, wlo_ok = (
            L.sem(f"{n}_p") for n in ("xh_done", "xhT_ok", "lg_done", "lg_ok", "whi_ok", "wlo_ok"))
        ident = G["const"][:, CC["ident"][0]:CC["ident"][1]]
        GROUPS = NT // RING

        def groups(eng, step):
            def body(g, lo, hi):
                for s in range(RING):
                    step(g, s, lambda k: lo <= s - k < hi)
            body(0, 0, RING)
            with eng.Fori(1, GROUPS) as g:
                body(g, -RING, RING)
            body(GROUPS, -RING, 0)

        def upto(g, s, back, per=1, plus=1):
            return g * (RING * per) + ((s - back) * per + plus)

        def slot(g, s, back, per=16):
            return g * per + ((s - back) // RING + 1) * per

        with nc.Block() as block:

            @block.sync
            def _(sp):
                sp.dma_start(wp[:, :, :], A["L0_xattn_Wp"].rearrange("(c p) n -> p c n", p=P)).then_inc(s_wp, 16)

                def step(g, s, live):
                    if live(0):
                        row = ds(g * (RING * P) + s * P, P)
                        after(sp, x1_ok, upto(g, s, 4))
                        sp.dma_start(at[:, s, :], A["attn"][row, :]).then_inc(ax_in[s], 16)
                        sp.dma_start(x[:, s, :], A["x"].rearrange("b s d -> (b s) d")[row, :]).then_inc(ax_in[s], 16)
                        after(sp, wlo_ok, upto(g, s, 4))
                        if s < DC:
                            src = A["L0_ffn_w1"][ds(g, 1), flat(s, P), :]
                            dst = w[:, s, :]
                        else:
                            src = A["L0_ffn_w2"][ds(g, 1), flat(s - DC, HID // 2), :].rearrange("e (m p) d -> p (e m) d", p=P)
                            dst = w[:, s, :].rearrange("p (m d) -> p m d", d=D)
                        sp.dma_start(dst, src).then_inc(w_in[s], 16)
                    if live(1):
                        k = (s - 1) % RING
                        row = ds(g * (RING * P) + (s - 1) * P, P)
                        sp.wait_ge(x1_ok, upto(g, s, 1))
                        sp.dma_start(A["x1"][row, :], x1[:, k, :]).then_inc(x1_out[k], 16)
                        sp.wait_ge(xh_ok, upto(g, s, 1))
                        sp.dma_start(A["xh"][row, :], xh[:, k, :]).then_inc(x1_out[k], 16)
                groups(sp, step)
                for k in range(RING):
                    sp.wait_ge(x1_out[k], 32 * GROUPS)

            @block.gpsimd
            def _(pool):
                def step(g, s, live):
                    if live(1):
                        k = (s - 1) % RING
                        pool.wait_ge(var_ok, upto(g, s, 1))
                        nc.gpsimd.tensor_tensor(rstd[:, k, :], ve[:, k, :], G["neghalf"][:, :], ALU.pow).then_inc(rstd_ok, 1)
                groups(pool, step)

            @block.tensor
            def _(pe):
                mm = nc.tensor.matmul
                pe.wait_ge(s_wp, 16)

                def step(g, s, live):
                    if live(0):
                        pe.wait_ge(ax_in[s], slot(g, s, 0, 32))
                        after(pe, atT_ok, upto(g, s, 1))
                        for c in range(DC):
                            last = nc.tensor.transpose(at_ps[:, flat(c, P)], at[:, s, flat(c, P)], ident)
                        last.then_inc(at_done, 1)
                    if live(1):
                        pe.wait_ge(atT_ok, upto(g, s, 1))
                        after(pe, x1_ok, upto(g, s, 2))
                        for c in range(DC):
                            last = mm(pr_ps[:, 0:D], atT[:, (s - 1) % 2, flat(c, P)], wp[:, c, :],
                                      start=c == 0, stop=c == DC - 1)
                        last.then_inc(pr_done, 1)
                    if live(2):
                        pe.wait_ge(xh_ok, upto(g, s, 2))
                        after(pe, xhT_ok, upto(g, s, 3))
                        for c in range(DC):
                            last = nc.tensor.transpose(xh_ps[:, flat(c, P)], xh[:, (s - 2) % RING, flat(c, P)], ident)
                        last.then_inc(xh_done, 1)
                    if live(3):
                        pe.wait_ge(xhT_ok, upto(g, s, 3))
                        after(pe, lg_ok, upto(g, s, 4))
                        for c in range(DC):
                            last = mm(lg_ps[:, 0:E], xhT[:, (s - 3) % 2, flat(c, P)], G["rwT"][:, c, :],
                                      start=c == 0, stop=c == DC - 1)
                        last.then_inc(lg_done, 1)
                groups(pe, step)

            @block.scalar
            def _(act):
                def step(g, s, live):
                    if live(0):
                        act.wait_ge(at_done, upto(g, s, 0))
                        after(act, pr_done, upto(g, s, 2))
                        nc.scalar.activation(atT[:, s % 2, :], at_ps[:, 0:D], ACT.Copy).then_inc(atT_ok, 1)
                        act.wait_ge(w_in[s], slot(g, s, 0))
                        nc.scalar.activation(G["experts"][:, ds(g * (8 * HID) + s * 2 * HID, HID)], w[:, s, :],
                                             ACT.Copy, scale=WSCALE).then_inc(whi_ok, 1)
                    if live(2):
                        act.wait_ge(xh_done, upto(g, s, 2))
                        after(act, lg_done, upto(g, s, 4))
                        nc.scalar.activation(xhT[:, s % 2, :], xh_ps[:, 0:D], ACT.Copy).then_inc(xhT_ok, 1)
                groups(act, step)

            @block.vector
            def _(dve):
                def step(g, s, live):
                    if live(1):
                        k = (s - 1) % RING
                        dve.wait_ge(pr_done, upto(g, s, 1))
                        after(dve, x1_out[k], slot(g, s, 5, 32))
                        nc.vector.tensor_tensor(x1[:, k, :], pr_ps[:, 0:D], x[:, k, :], ALU.add).then_inc(x1_ok, 1)
                        dve.wait_ge(x1_ok, upto(g, s, 1))
                        normed(nc, dve, x1[:, k, :], stats[:, k, :], mv[:, k, :], ve[:, k, :], ch, upto(g, s, 1, 2, 0), var_ok,
                               G["dve_passed"])
                    if live(0):
                        hi = g * (8 * HID) + s * 2 * HID
                        dve.wait_ge(whi_ok, upto(g, s, 0))
                        nc.vector.scalar_tensor_tensor(G["experts"][:, ds(hi + HID, HID)], w[:, s, :], WSCALE,
                                                       G["experts"][:, ds(hi, HID)], ALU.mult, ALU.subtract).then_inc(wlo_ok, 1)
                    if live(1):
                        k = (s - 1) % RING
                        dve.wait_ge(rstd_ok, upto(g, s, 1))
                        nc.vector.tensor_scalar(xh[:, k, :], x1[:, k, :], mv[:, k, 0:1], rstd[:, k, :],
                                                ALU.subtract, ALU.mult).then_inc(xh_ok, 1)
                    if live(3):
                        dve.wait_ge(lg_done, upto(g, s, 3))
                        nc.vector.tensor_scalar(G["logits"][:, ds(g * RING + (s - 3), 1), :], lg_ps[:, None, 0:E],
                                                1.0, None, ALU.mult) \
                            .then_inc(lg_ok, 1)
                groups(dve, step)


def route(nc, A, G):
    Q = NT // 4
    with ExitStack() as ctx:
        L = Place(nc, ctx)
        te, et = [P, NT, E], [P, E, NT]
        mx, z, v1, v2, f1, f2, den = (L.sb(f"{n}_r", [P, NT]) for n in ("mx", "z", "v1", "v2", "f1", "f2", "den"))
        ex, pr, eq, pr2 = (L.sb(f"{n}_r", te) for n in ("ex", "pr", "eq", "pr2"))
        m1, m2 = L.sb("m1_r", te), L.sb("m2_r", te)
        both = L.sb("both_r", et, F16)
        tot, inc, pos, tmp = (L.sb(f"{n}_r", et) for n in ("tot", "inc", "pos", "tmp"))
        nb, ends, base = (L.sb(f"{n}_r", [P, E]) for n in ("nb", "ends", "base"))
        nbi = L.sb("nbi_r", [P, E], I32)
        ones = L.sb("ones_r", [P, E])
        slotf = L.sb("slotf_r", [P, NT, 2])
        sloti = L.sb("sloti_r", [P, NT, 2], I32)
        hi_i = L.sb("hi_i_r", [P, NT, 2], I32)
        hi_f, lo_f = L.sb("hi_f_r", [P, NT, 2]), L.sb("lo_f_r", [P, NT, 2])
        cmp_, cnt = L.sb("cmp_r", [1, ET, E]), L.sb("cnt_r", [1, ET])
        rowhot = L.sb("rowhot_r", [P, 2, Q, 2, P], F16)
        halfhot = L.sb("halfhot_r", [P, 2, Q, 2, HALFT], F16)
        tokhot = L.sb("tokhot_r", [P, 2, Q, 2, 2, HALFT], F16)
        tab = L.sb("tab_r", [P, HALFT])
        rank_ps, tot_ps, tab_ps = L.bank("rank_ps"), L.bank("tot_ps"), L.bank("tab_ps")
        ch, s_shift, s_exp, s_both, s_cnt, s_hot, s_place, s_tile, s_tab = (
            L.sem(f"{n}_r") for n in ("ch", "shift", "exp", "both", "cnt", "hot", "place", "tile", "tab"))
        col = lambda n: G["const"][:, CC[n][0]:CC[n][1]]
        with nc.Block() as block:

            @block.scalar
            def _(act):
                act.wait_ge(s_shift, 1)
                nc.scalar.activation(ex[:, :, :], pr2[:, :, :], ACT.Exp).then_inc(s_exp, 1)
                for q in range(4):
                    act.wait_ge(s_hot, 2 * q + 2)
                    after(act, s_tab, q - 1)
                    nc.scalar.activation(tokhot[:, q % 2, :, :, 1, :], halfhot[:, q % 2, :, :, :], ACT.Copy,
                                         scale=col("part")).then_inc(s_place, 1)

            @block.tensor
            def _(pe):
                mm = nc.tensor.matmul
                pe.wait_ge(s_both, 1)
                m = both[:, :, :].rearrange("p e t -> p (e t)")
                mm(rank_ps[:, 0:E * NT], G["tri16"][:, :], m, start=True, stop=True)
                mm(tot_ps[:, 0:E * NT], G["ones16"][:, :], m, start=True, stop=True).then_inc(s_cnt, 1)
                for q in range(4):
                    pe.wait_ge(s_place, q + 1)
                    pe.wait_ge(s_tile, q + 1)
                    for t in range(q * Q, (q + 1) * Q):
                        for c in range(2):
                            last = mm(tab_ps[:, 0:2 * HALFT], rowhot[:, q % 2, t % Q, c, :],
                                      tokhot[:, q % 2, t % Q, c, :, :].rearrange("p a h -> p (a h)"),
                                      start=t == 0 and c == 0, stop=t == NT - 1 and c == 1)
                    last.then_inc(s_tab, 1)

            @block.vector
            def _(dve):
                count = [0]

                def link(ins):
                    count[0] += 1
                    ins.then_inc(ch, 1)
                    dve.wait_ge(ch, count[0])

                v = nc.vector
                lg = G["logits"]
                wide = lambda a: a[:, :, None].broadcast_to(te)
                link(v.tensor_reduce(mx[:, :], lg[:, :, :], AX.X, ALU.max))
                v.tensor_tensor(pr2[:, :, :], lg[:, :, :], wide(mx), ALU.subtract).then_inc(s_shift, 1)
                dve.wait_ge(s_exp, 1)
                link(v.tensor_reduce(z[:, :], ex[:, :, :], AX.X, ALU.add))
                link(v.reciprocal(mx[:, :], z[:, :]))
                link(v.tensor_tensor(pr[:, :, :], ex[:, :, :], wide(mx), ALU.mult))
                rank8 = col("rank8")[:, None, :].broadcast_to(te)

                def largest(p, val, f, m):
                    link(v.tensor_reduce(val[:, :], p[:, :, :], AX.X, ALU.max))
                    link(v.tensor_tensor(eq[:, :, :], p[:, :, :], wide(val), ALU.is_equal))
                    link(v.tensor_tensor(eq[:, :, :], eq[:, :, :], rank8, ALU.mult))
                    link(v.tensor_reduce(f[:, :], eq[:, :, :], AX.X, ALU.max))
                    link(v.tensor_tensor(m[:, :, :], rank8, wide(f), ALU.is_equal))

                largest(pr, v1, f1, m1)
                link(v.scalar_tensor_tensor(pr2[:, :, :], m1[:, :, :], -2.0, pr[:, :, :], ALU.mult, ALU.add))
                largest(pr2, v2, f2, m2)
                v.tensor_tensor(both[:, :, :].rearrange("p e t -> p t e"), m1[:, :, :], m2[:, :, :], ALU.add).then_inc(s_both, 1)
                link(v.tensor_tensor(den[:, :], v1[:, :], v2[:, :], ALU.add))
                link(v.tensor_scalar(den[:, :], den[:, :], 1e-9, None, ALU.add))
                link(v.reciprocal(z[:, :], den[:, :]))
                for n, val in enumerate((v1, v2)):
                    v.tensor_tensor(G["cw_t"][:, :, n, :].rearrange("p s b -> p b s"),
                                    val[:, :].rearrange("p (b s) -> p b s", b=B),
                                    z[:, :].rearrange("p (b s) -> p b s", b=B), ALU.mult)
                v.memset(ones[:, :], 1.0)
                dve.wait_ge(s_cnt, 1)
                link(v.tensor_copy(tot[:, :, :], tot_ps[:, 0:E * NT].rearrange("p (e t) -> p e t", e=E)))
                fl = lambda a: a[:, :, :].rearrange("p e t -> p (e t)")
                link(v.tensor_tensor_scan(fl(inc), col("restart"), fl(tot), 0.0, ALU.mult, ALU.add))
                link(v.tensor_scalar(nb[:, :], inc[:, :, NT - 1], float(SLOTS - 1), None, ALU.add))
                link(v.tensor_copy(nbi[:, :], nb[:, :]))
                link(v.tensor_scalar(nbi[:, :], nbi[:, :], SLOTS.bit_length() - 1, None, ALU.arith_shift_right))
                link(v.tensor_copy(nb[:, :], nbi[:, :]))
                link(v.tensor_tensor_scan(ends[:, :], ones[:, :], nb[:, :], 0.0, ALU.mult, ALU.add))
                link(v.tensor_tensor(base[:, :], ends[:, :], nb[:, :], ALU.subtract))
                link(v.tensor_scalar(base[:, :], base[:, :], float(SLOTS), None, ALU.mult))
                link(v.tensor_tensor(pos[:, :, :], inc[:, :, :], tot[:, :, :], ALU.subtract))
                link(v.tensor_tensor(pos[:, :, :], pos[:, :, :],
                                     rank_ps[:, 0:E * NT].rearrange("p (e t) -> p e t", e=E), ALU.add))
                link(v.tensor_tensor(pos[:, :, :], pos[:, :, :], base[:, :, None].broadcast_to(et), ALU.add))
                for n, m in enumerate((m1, m2)):
                    link(v.tensor_tensor(tmp[:, :, :], pos[:, :, :], m[:, :, :].rearrange("p t e -> p e t"), ALU.mult))
                    link(v.tensor_reduce(slotf[:, :, n], tmp[:, :, :].rearrange("p e t -> p t e"), AX.X, ALU.add))
                link(v.tensor_copy(sloti[:, :, :], slotf[:, :, :]))
                v.tensor_copy(G["slots_t"][:, :, :, :], sloti[:, :, :].rearrange("p (b s) n -> p s n b", b=B))
                link(v.tensor_scalar(hi_i[:, :, :], sloti[:, :, :], 7, None, ALU.arith_shift_right))
                link(v.tensor_copy(hi_f[:, :, :], hi_i[:, :, :]))
                link(v.scalar_tensor_tensor(lo_f[:, :, :], hi_f[:, :, :], -float(P), slotf[:, :, :], ALU.mult, ALU.add))
                for q in range(4):
                    part = flat(q, Q)
                    after(dve, s_tab, q - 1)
                    after(dve, s_place, q - 1)
                    v.tensor_tensor(rowhot[:, q % 2, :, :, :].rearrange("p t c r -> p (t c) r"),
                                    col("rowid")[:, None, :].broadcast_to([P, 2 * Q, P]),
                                    lo_f[:, part, :].rearrange("p t c -> p (t c)")[:, :, None].broadcast_to([P, 2 * Q, P]),
                                    ALU.is_equal).then_inc(s_hot, 1)
                    v.tensor_tensor(halfhot[:, q % 2, :, :, :].rearrange("p t c r -> p (t c) r"),
                                    col("halfid")[:, None, :].broadcast_to([P, 2 * Q, HALFT]),
                                    hi_f[:, part, :].rearrange("p t c -> p (t c)")[:, :, None].broadcast_to([P, 2 * Q, HALFT]),
                                    ALU.is_equal).then_inc(s_hot, 1)
                    dve.wait_ge(s_hot, 2 * q + 2)
                    v.tensor_tensor(tokhot[:, q % 2, :, :, 0, :], halfhot[:, q % 2, :, :, :],
                                    col("tileid")[:, part, None, None].broadcast_to([P, Q, 2, HALFT]), ALU.mult).then_inc(s_tile, 1)
                link(v.tensor_scalar(ends[:, :], ends[:, :], float(SLOTS), None, ALU.mult))
                link(v.tensor_tensor(cmp_[:, :, :], col("slot0")[0:1, :, None].broadcast_to([1, ET, E]),
                                     ends[0:1, None, :].broadcast_to([1, ET, E]), ALU.is_ge))
                link(v.tensor_reduce(cnt[:, :], cmp_[:, :, :], AX.X, ALU.add))
                link(v.tensor_scalar(cnt[:, :], cnt[:, :], float(E - 1), None, ALU.min))
                v.tensor_copy(G["tile_expert"][:, :], cnt[:, :])
                dve.wait_ge(s_tab, 4)
                link(v.tensor_scalar(tab[:, :], tab_ps[:, 0:HALFT], float(P), None, ALU.mult))
                link(v.tensor_tensor(tab[:, :], tab[:, :], tab_ps[:, HALFT:2 * HALFT], ALU.add))
                v.tensor_copy(G["token"][:, :], tab[:, :])


def experts(nc, A, G):
    with ExitStack() as ctx:
        L = Place(nc, ctx)
        idx = L.sb("idx_e", [P, 2], I32)
        x = L.sb("x_e", [P, 2, D])
        xT = [L.sb(f"xT_e{i}", [P, DC, SLOTS], F16) for i in range(2)]
        h = L.sb("h_e", [P, 2, 2 * SLOTS])
        hh = [L.sb(f"hh_e{i}", [P, 2, 2 * SLOTS], F16) for i in range(2)]
        y = L.sb("y_e", [P, 2, D])
        xT_ps = L.bank("xT_ps_e")
        up_ps = [L.bank(f"up_ps{i}") for i in range(4)]
        y_ps = [L.bank(f"y_ps{i}") for i in range(2)]
        idx_ok, x_in, xT_done, xhi_ok, xlo_ok, up_done = (
            L.sem(f"{n}_e") for n in ("idx_ok", "x_in", "xT_done", "xhi_ok", "xlo_ok", "up_done"))
        gelu_ok, hhi_ok, hlo_ok, down_done, y_done, y_ok, y_out = (
            L.sem(f"{n}_e") for n in ("gelu_ok", "hhi_ok", "hlo_ok", "down_done", "y_done", "y_ok", "y_out"))
        ident = G["const"][:, CC["ident"][0]:CC["ident"][1]]
        QS = 4

        def tiles(eng, step):
            step(0, True)
            with eng.Fori(1, ET - 1) as k:
                step(k, True)
            step(ET - 1, False)

        with nc.Block() as block:

            @block.gpsimd
            def _(pool):
                def step(k, more):
                    after(pool, xT_done, k)
                    nc.gpsimd.tensor_copy(idx[:, :], G["token"][:, ds(k * 2, 2)]).then_inc(idx_ok, 1)
                    apart(pool, idx_ok, k + 1, G["pool_passed"])
                    for n in range(2):
                        pool.indirect_dma_start(out=x[:, n, :], out_offset=None, in_=A["xh"],
                                                in_offset=bass.IndirectOffsetOnAxis(ap=idx[:, n:n + 1], axis=0)) \
                            .then_inc(x_in, 16)
                tiles(pool, step)

            @block.sync
            def _(sp):
                def step(k, more):
                    sp.wait_ge(y_ok, 2 * k + 2)
                    sp.dma_start(A["y"][ds(k * SLOTS, SLOTS), :].rearrange("(n p) d -> p n d", p=P), y[:, :, :]) \
                        .then_inc(y_out, 16)
                tiles(sp, step)
                sp.wait_ge(y_out, 16 * ET)

            @block.tensor
            def _(pe):
                mm = nc.tensor.matmul

                def transpose(k):
                    pe.wait_ge(x_in, k * 32 + 32)
                    after(pe, xlo_ok, k)
                    for c in range(DC):
                        for n in range(2):
                            last = nc.tensor.transpose(xT_ps[:, ds(c * SLOTS + n * P, P)], x[:, n, flat(c, P)], ident)
                    last.then_inc(xT_done, 1)

                def step(k, more):
                    expert = pe.value_load(G["tile_expert"][0:1, ds(k, 1)], min_val=0, max_val=E - 1)
                    at = pe.snap(expert * (8 * HID))
                    W = G["experts"]

                    def up(q):
                        after(pe, gelu_ok, k * QS + q - 3)
                        for m in (2 * q, 2 * q + 1):
                            out = up_ps[q][:, flat(m % 2, SLOTS)]
                            for c in range(DC):
                                w = [W[:, ds(at + (c * 2 * HID + half * HID + m * P), P)] for half in range(2)]
                                mm(out, w[0], xT[0][:, c, :], start=c == 0, stop=False)
                                mm(out, w[0], xT[1][:, c, :], start=False, stop=False)
                                last = mm(out, w[1], xT[0][:, c, :], start=False, stop=c == DC - 1)
                        last.then_inc(up_done, 1)

                    def down(q):
                        pe.wait_ge(hlo_ok, k * QS + q + 1)
                        if q == 0:
                            after(pe, y_ok, 2 * k)
                        for m in (2 * q, 2 * q + 1):
                            w = [W[:, ds(at + ((2 + m // 4) * 2 * HID + half * HID + m % 4 * D), D)] for half in range(2)]
                            for n in range(2):
                                a = [hh[half][:, q % 2, ds(m % 2 * SLOTS + n * P, P)] for half in range(2)]
                                out = y_ps[n][:, 0:D]
                                mm(out, a[0], w[0], start=m == 0, stop=False)
                                mm(out, a[0], w[1], start=False, stop=False)
                                last = mm(out, a[1], w[0], start=False, stop=m == 7)
                        last.then_inc(down_done, 1)

                    pe.wait_ge(xlo_ok, k + 1)
                    up(0)
                    up(1)
                    down(0)
                    up(2)
                    down(1)
                    up(3)
                    if more:
                        transpose(k + 1)
                    down(2)
                    down(3)

                transpose(0)
                tiles(pe, step)

            @block.scalar
            def _(act):
                def rows(k):
                    act.wait_ge(xT_done, k + 1)
                    after(act, up_done, k * QS)
                    nc.scalar.activation(xT[0][:, :, :], xT_ps[:, :].rearrange("p (c t) -> p c t", c=DC), ACT.Copy) \
                        .then_inc(xhi_ok, 1)

                def step(k, more):
                    for q in range(QS):
                        act.wait_ge(up_done, k * QS + q + 1)
                        after(act, hlo_ok, k * QS + q - 1)
                        nc.scalar.activation(h[:, q % 2, :], up_ps[q][:, :], ACT.Gelu, scale=1 / WSCALE).then_inc(gelu_ok, 1)
                    if more:
                        rows(k + 1)
                    act.wait_ge(down_done, k * QS + QS)
                    after(act, y_out, k * 16)
                    for n in range(2):
                        nc.scalar.activation(y[:, n, :], y_ps[n][:, 0:D], ACT.Copy, scale=1 / WSCALE).then_inc(y_ok, 1)

                rows(0)
                tiles(act, step)

            @block.vector
            def _(dve):
                def rows(k):
                    dve.wait_ge(xhi_ok, k + 1)
                    nc.vector.tensor_tensor(xT[1][:, :, :], xT_ps[:, :].rearrange("p (c t) -> p c t", c=DC),
                                            xT[0][:, :, :], ALU.subtract).then_inc(xlo_ok, 1)

                def step(k, more):
                    for q in range(QS):
                        dve.wait_ge(gelu_ok, k * QS + q + 1)
                        after(dve, down_done, k * QS + q - 1)
                        nc.vector.tensor_copy(hh[0][:, q % 2, :], h[:, q % 2, :]).then_inc(hhi_ok, 1)
                        dve.wait_ge(hhi_ok, k * QS + q + 1)
                        nc.vector.tensor_tensor(hh[1][:, q % 2, :], h[:, q % 2, :], hh[0][:, q % 2, :], ALU.subtract) \
                            .then_inc(hlo_ok, 1)
                    if more:
                        rows(k + 1)

                rows(0)
                tiles(dve, step)


def feed_forward(nc, A, G):
    U = 4 * P
    with ExitStack() as ctx:
        L = Place(nc, ctx)
        at = L.sb("at_f", [P, 4, D])
        x2 = L.sb("x2_f", [P, 4, D])
        atT = L.sb("atT_f", [P, 2, D])
        x3 = L.sb("x3_f", [P, 8, D])
        xh = L.sb("xh_f", [P, 4, D])
        xhT = L.sb("xhT_f", [P, 2, DC, U])
        stats, mv = L.sb("stats_f", [P, 4, 6]), L.sb("mv_f", [P, 4, 2])
        ve, rstd = L.sb("ve_f", [P, 4, 1]), L.sb("rstd_f", [P, 4, 1])
        bo = L.sb("bo_f", [P, D])
        u1 = L.sb("u1_f", [P, DC, RANK])
        w1 = L.sb("v1_f", [RANK, HID])
        b1 = L.sb("b1_f", [P, HID // P])
        u2 = L.sb("u2_f", [P, HID // P, RANK])
        w2 = L.sb("v2_f", [RANK + 1, D])
        low = L.sb("low_f", [RANK, U])
        h = L.sb("h_f", [P, 2, U])
        low2 = L.sb("low2_f", [RANK + 1, U])
        out = L.sb("out_f", [P, 4, D])
        at_ps, pr_ps, xh_ps, low_ps, low2_ps, out_ps = (L.bank(f"{n}_ps_f") for n in ("at", "pr", "xh", "low", "low2", "out"))
        h_ps = [L.bank(f"h_ps{i}_f") for i in range(2)]
        w_in = L.sem("w_in_f")
        ax_in = [L.sem(f"ax_in{i}_f") for i in range(4)]
        res_out = [L.sem(f"res_out{i}") for i in range(4)]
        at_done, atT_ok, pr_done, x3a_ok, x3_ok, ch, var_ok, rstd_ok, xh_ok, xh_done, xhT_ok = (
            L.sem(f"{n}_f") for n in ("at_done", "atT_ok", "pr_done", "x3a_ok", "x3_ok", "ch", "var_ok", "rstd_ok", "xh_ok",
                                      "xh_done", "xhT_ok"))
        low_done, low_ok, h_done, h_ok, back_done, low2_ok, out_done, out_ok = (
            L.sem(f"{n}_f") for n in ("low_done", "low_ok", "h_done", "h_ok", "back_done", "low2_ok", "out_done", "out_ok"))
        ident = G["const"][:, CC["ident"][0]:CC["ident"][1]]
        MS = HID // P
        LOADS = 7

        def bodies(eng, step):
            def body(bb, lo, hi):
                for s in range(TB):
                    step(bb, s, lambda k: lo <= s - k < hi)
            body(0, 0, TB)
            with eng.Fori(1, B) as bb:
                body(bb, -TB, TB)
            body(B, -TB, 0)

        def upto(bb, s, back, per=1, plus=1):
            return bb * (TB * per) + ((s - back) * per + plus)

        def slot(bb, s, back, per=16):
            return bb * (2 * per) + ((s - back) // 4 + 1) * per

        def phase(s):
            return (s + 2) % 4

        def unit(bb, s, per=1, plus=0):
            return bb * (2 * per) + ((s - 6 - phase(s)) // 4 * per + plus)

        SCHEDULE = {0: ["low", ("h", 0), ("h", 1), ("b", 0), ("h", 2), ("b", 1)],
                    1: [("h", 3), ("b", 2), ("h", 4), ("b", 3), ("h", 5), ("b", 4)],
                    2: [("h", 6), ("b", 5), ("h", 7), ("b", 6), ("b", 7)],
                    3: ["out"]}

        with nc.Block() as block:

            @block.sync
            def _(sp):
                sp.dma_start(bo[:, :], A["L1_xattn_bo"][None, :].broadcast_to([P, D])).then_inc(w_in, 16)
                sp.dma_start(u1[:, :, :], A["L1_ffn_U1"].rearrange("(c p) r -> p c r", p=P)).then_inc(w_in, 16)
                sp.dma_start(w1[:, :], A["L1_ffn_V1"]).then_inc(w_in, 16)
                with nc.allow_non_contiguous_dma(reason="a thousand biases, onto partitions"):
                    sp.dma_start(b1[:, :], A["L1_ffn_b1"].rearrange("(m p) -> p m", p=P)).then_inc(w_in, 16)
                sp.dma_start(u2[:, :, :], A["L1_ffn_U2"].rearrange("(m p) r -> p m r", p=P)).then_inc(w_in, 16)
                sp.dma_start(w2[0:RANK, :], A["L1_ffn_V2"]).then_inc(w_in, 16)
                sp.dma_start(w2[RANK:RANK + 1, :], A["L1_ffn_b2"][None, :]).then_inc(w_in, 16)

                def step(bb, s, live):
                    if live(0):
                        row = ds(bb * S + s * P, P)
                        after(sp, x3a_ok, upto(bb, s, 4))
                        sp.dma_start(at[:, s % 4, :], A["attn1"][row, :]).then_inc(ax_in[s % 4], 16)
                        sp.dma_start(x2[:, s % 4, :], A["x2"][row, :]).then_inc(ax_in[s % 4], 16)
                    ph = phase(s)
                    if ph == 3 and live(9):
                        for i in range(4):
                            row = ds(bb * S + (s - 9 + i) * P, P)
                            sp.wait_ge(out_ok, unit(bb, s, 4, i + 1))
                            sp.dma_start(A["out"].rearrange("b s d -> (b s) d")[row, :], out[:, i, :]).then_inc(res_out[i], 16)
                bodies(sp, step)
                for i in range(4):
                    sp.wait_ge(res_out[i], 16 * NT // 4)

            @block.gpsimd
            def _(pool):
                def step(bb, s, live):
                    if live(1):
                        k = (s - 1) % 4
                        pool.wait_ge(var_ok, upto(bb, s, 1))
                        nc.gpsimd.tensor_tensor(rstd[:, k, :], ve[:, k, :], G["neghalf"][:, :], ALU.pow).then_inc(rstd_ok, 1)
                bodies(pool, step)

            @block.tensor
            def _(pe):
                mm = nc.tensor.matmul
                pe.wait_ge(w_in, 16 * LOADS)

                def step(bb, s, live):
                    if live(0):
                        pe.wait_ge(ax_in[s % 4], slot(bb, s, 0, 32))
                        after(pe, atT_ok, upto(bb, s, 1))
                        for c in range(DC):
                            last = nc.tensor.transpose(at_ps[:, flat(c, P)], at[:, s % 4, flat(c, P)], ident)
                        last.then_inc(at_done, 1)
                    ph = phase(s)
                    if live(6 + ph):
                        par = (s - 6 - ph) % TB // 4
                        for item in SCHEDULE[ph]:
                            if item == "low":
                                pe.wait_ge(xhT_ok, unit(bb, s, 4, 4))
                                after(pe, low_ok, unit(bb, s))
                                for c in range(DC):
                                    last = mm(low_ps[0:RANK, :], u1[:, c, :], xhT[:, par, c, :], start=c == 0, stop=c == DC - 1)
                                last.then_inc(low_done, 1)
                            elif item == "out":
                                pe.wait_ge(low2_ok, unit(bb, s, 1, 1))
                                for i in range(4):
                                    after(pe, out_ok, unit(bb, s, 4, i))
                                    mm(out_ps[:, 0:D], low2[:, flat(i, P)], w2[:, :], start=True, stop=True).then_inc(out_done, 1)
                            elif item[0] == "h":
                                m = item[1]
                                if m == 0:
                                    pe.wait_ge(low_ok, unit(bb, s, 1, 1))
                                after(pe, h_ok, unit(bb, s, MS, m - 1))
                                mm(h_ps[m % 2][:, :], w1[:, flat(m, P)], low[:, :], start=True, stop=True).then_inc(h_done, 1)
                            else:
                                m = item[1]
                                pe.wait_ge(h_ok, unit(bb, s, MS, m + 1))
                                if m == 0:
                                    after(pe, low2_ok, unit(bb, s))
                                mm(low2_ps[0:RANK, :], u2[:, m, :], h[:, m % 2, :], start=m == 0, stop=m == MS - 1) \
                                    .then_inc(back_done, 1)
                    if live(1):
                        pe.wait_ge(atT_ok, upto(bb, s, 1))
                        after(pe, x3a_ok, upto(bb, s, 2))
                        for c in range(DC):
                            last = mm(pr_ps[:, 0:D], atT[:, (s - 1) % 2, flat(c, P)], G["woT"][:, c, :],
                                      start=c == 0, stop=c == DC - 1)
                        last.then_inc(pr_done, 1)
                    if live(2):
                        pe.wait_ge(xh_ok, upto(bb, s, 2))
                        after(pe, xhT_ok, upto(bb, s, 3))
                        for c in range(DC):
                            last = nc.tensor.transpose(xh_ps[:, flat(c, P)], xh[:, (s - 2) % 4, flat(c, P)], ident)
                        last.then_inc(xh_done, 1)
                bodies(pe, step)

            @block.scalar
            def _(act):
                act.wait_ge(w_in, 16 * LOADS)

                def step(bb, s, live):
                    if live(0):
                        act.wait_ge(at_done, upto(bb, s, 0))
                        after(act, pr_done, upto(bb, s, 2))
                        nc.scalar.activation(atT[:, s % 2, :], at_ps[:, 0:D], ACT.Copy).then_inc(atT_ok, 1)
                    ph = phase(s)
                    if live(6 + ph):
                        for item in SCHEDULE[ph]:
                            if item == "low":
                                act.wait_ge(low_done, unit(bb, s, 1, 1))
                                after(act, h_done, unit(bb, s, MS))
                                nc.scalar.activation(low[:, :], low_ps[0:RANK, :], ACT.Copy).then_inc(low_ok, 1)
                            elif item[0] == "h":
                                m = item[1]
                                act.wait_ge(h_done, unit(bb, s, MS, m + 1))
                                after(act, back_done, unit(bb, s, MS, m - 1))
                                nc.scalar.activation(h[:, m % 2, :], h_ps[m % 2][:, :], ACT.Gelu_apprx_tanh,
                                                     bias=b1[:, m:m + 1]).then_inc(h_ok, 1)
                    if live(2):
                        k = (s - 2) % TB
                        act.wait_ge(xh_done, upto(bb, s, 2))
                        if k % 4 == 0:
                            after(act, low_done, bb * 2 + ((s - 2) // 4 - 1))
                        nc.scalar.activation(xhT[:, k // 4, :, flat(k % 4, P)],
                                             xh_ps[:, 0:D].rearrange("p (c t) -> p c t", c=DC), ACT.Copy).then_inc(xhT_ok, 1)
                bodies(act, step)

            @block.vector
            def _(dve):
                nc.vector.memset(low2[RANK:RANK + 1, :], 1.0)
                dve.wait_ge(w_in, 16 * LOADS)

                def step(bb, s, live):
                    ph = phase(s)
                    if ph == 3 and live(9):
                        for i in range(4):
                            dve.wait_ge(out_done, unit(bb, s, 4, i + 1))
                            after(dve, res_out[i], unit(bb, s, 16))
                            nc.vector.tensor_tensor(out[:, i, :], out_ps[:, 0:D], x3[:, (s - 9) % TB + i, :], ALU.add) \
                                .then_inc(out_ok, 1)
                    if live(1):
                        k = (s - 1) % 4
                        dve.wait_ge(pr_done, upto(bb, s, 1))
                        nc.vector.tensor_tensor(x3[:, (s - 1) % TB, :], pr_ps[:, 0:D], x2[:, k, :], ALU.add).then_inc(x3a_ok, 1)
                        dve.wait_ge(x3a_ok, upto(bb, s, 1))
                        nc.vector.tensor_tensor(x3[:, (s - 1) % TB, :], x3[:, (s - 1) % TB, :], bo[:, :], ALU.add).then_inc(x3_ok, 1)
                        dve.wait_ge(x3_ok, upto(bb, s, 1))
                        normed(nc, dve, x3[:, (s - 1) % TB, :], stats[:, k, :], mv[:, k, :], ve[:, k, :], ch,
                               upto(bb, s, 1, 2, 0), var_ok, G["dve_passed"])
                        dve.wait_ge(rstd_ok, upto(bb, s, 1))
                        after(dve, xh_done, upto(bb, s, 5))
                        nc.vector.tensor_scalar(xh[:, k, :], x3[:, (s - 1) % TB, :], mv[:, k, 0:1], rstd[:, k, :],
                                                ALU.subtract, ALU.mult).then_inc(xh_ok, 1)
                    if ph == 2 and live(8):
                        dve.wait_ge(back_done, unit(bb, s, MS, MS))
                        after(dve, out_done, unit(bb, s, 4))
                        nc.vector.tensor_copy(low2[0:RANK, :], low2_ps[0:RANK, :]).then_inc(low2_ok, 1)
                bodies(dve, step)


def program(nc, A):
    for name, shape in (("values0", [B, KEYS * D]), ("attn", [B * S, D]), ("x1", [B * S, D]), ("xh", [B * S, D]),
                        ("y", [ET * SLOTS, D]), ("x2", [B * S, D]), ("attn1", [B * S, D])):
        A[name] = nc.dram_tensor(name + "_scratch", shape, F32).ap()
    with ExitStack() as ctx:
        G = allocate(nc, ctx)
        with ExitStack() as inner:
            allocate_first(nc, inner, G)
            prepare(nc, A, G)
            attention(nc, A, G, 0)
        with ExitStack() as inner:
            G["experts"] = Place(nc, inner).sb("experts", [P, E * 8 * HID], F16)
            project(nc, A, G)
            route(nc, A, G)
            experts(nc, A, G)
        attention(nc, A, G, 1)
        feed_forward(nc, A, G)


_INS = ["x", "ctx_1024", "L0_xattn_Wq", "L0_xattn_Wk", "L0_xattn_Wv", "L0_xattn_Wp", "L0_ffn_router_w", "L0_ffn_w1",
        "L0_ffn_w2", "L1_xattn_Wv", "L1_xattn_Wk", "L1_xattn_Wq", "L1_xattn_Wo", "L1_xattn_bo", "L1_ffn_U1", "L1_ffn_V1",
        "L1_ffn_b1", "L1_ffn_U2", "L1_ffn_V2", "L1_ffn_b2"]


def kernel(**inputs):
    import concourse.bacc as bacc
    from concourse.bass_utils import run_bass_kernel_spmd as run

    nc = bacc.Bacc("TRN2", target_bir_lowering=False, num_devices=1)
    arrays, args = {}, {}
    for name in _INS + ["const"]:
        a = np.ascontiguousarray(constants() if name == "const" else inputs[name])
        arrays[f"in_{name}"] = a
        args[name] = nc.dram_tensor(f"in_{name}", a.shape, mybir.dt.from_np(a.dtype), kind="ExternalInput").ap()
    args["out"] = nc.dram_tensor("out_0", (B, S, D), F32, kind="ExternalOutput").ap()
    program(nc, args)
    r = run(nc, [arrays], core_ids=[0])
    return r.results[0]["out_0"]
```

```python
import numpy as np
import concourse.bass as bass
from concourse import mybir
from contextlib import ExitStack

F32 = mybir.dt.float32
F16 = mybir.dt.float16
BF16 = mybir.dt.bfloat16
I32 = mybir.dt.int32
ACT = mybir.ActivationFunctionType
ALU = mybir.AluOpType
AX = mybir.AxisListType
ds = bass.ds

P = 128
B, S, D = 4, 1024, 256
KEYS = 77
HEADS = 16
HD = D // HEADS
NT = B * S // P
TB = S // P
DC = D // P
HK = HEADS * KEYS
CH = 4 * KEYS
VW = HD + 1
HR = 4 * HD
E, HID = 8, 1024
SLOTS = 256
ET = (2 * B * S + E * (SLOTS - 1)) // SLOTS
HALFT = ET * SLOTS // P
WSCALE = 64.0
MSCALE = 64.0
RANK = 64
EPS = 1e-5
NEG = -1e30

CC = {}
_at = 0
for _n, _w in (("ident", P), ("tri", P), ("rowid", P), ("halfid", HALFT), ("blocks", P // HD),
               ("rows", 3), ("early", P), ("latekeys", HEADS * KEYS), ("seen", HEADS * 5),
               ("part", 1), ("restart", E * NT), ("tileid", NT), ("rank8", E), ("slot0", ET)):
    CC[_n] = (_at, _at + _w)
    _at += _w
CW = _at


def constants():
    c = np.zeros((P, CW), np.float32)

    def put(name, v):
        a, b = CC[name]
        v = np.asarray(v, np.float32)
        c[:v.shape[0], a:b] = v.reshape(v.shape[0], b - a)

    p = np.arange(P)
    put("ident", np.eye(P))
    put("tri", p[:, None] < p[None, :])
    put("rowid", np.broadcast_to(p, (P, P)))
    put("halfid", np.broadcast_to(np.arange(HALFT), (P, HALFT)))
    put("blocks", p[:, None] // HD == np.arange(P // HD)[None, :])
    w = p % HR
    put("rows", np.stack([w < 2 * HD, (w >= 2 * HD) & (w < 3 * HD),
                          MSCALE * ((w == 3 * HD) | (w == 3 * HD + 1))], 1))
    i = np.arange(5)
    put("early", i[:, None] == p[None, :] % 64)
    j, k = np.arange(HEADS), np.arange(KEYS)
    put("latekeys", NEG * (k[None, None, :] > 16 * i[:, None, None] + j[None, :, None]))
    rj = (2 * np.arange(8)[None, :] + np.arange(2)[:, None]).reshape(-1)
    put("seen", k[:, None, None] <= 16 * i[None, None, :] + rj[None, :, None])
    put("part", p[:, None])
    put("restart", np.broadcast_to((np.arange(E * NT) % NT != 0), (P, E * NT)))
    put("tileid", np.broadcast_to(np.arange(NT), (P, NT)))
    put("rank8", np.broadcast_to(E - np.arange(E), (P, E)))
    put("slot0", np.broadcast_to(SLOTS * np.arange(ET), (P, ET)))
    return c


def flat(i, n):
    return slice(i * n, (i + 1) * n)


def after(eng, sem, value):
    if isinstance(value, int) and value <= 0:
        return
    eng.wait_ge(sem, value)


def apart(eng, sem, value, passed):
    eng.wait_ge(sem, value)
    if not isinstance(value, int):
        eng.sem_inc(passed, 1)


class Place:

    def __init__(self, nc, ctx):
        self.nc, self.ctx = nc, ctx

    def sb(self, name, shape, dt=F32):
        return self.ctx.enter_context(self.nc.sbuf_tensor(name, shape, dt))

    def bank(self, name, dt=F32):
        return self.ctx.enter_context(self.nc.psum_tensor(name, [P, 2048 // (4 if dt == F32 else 2)], dt))

    def sem(self, name):
        return self.ctx.enter_context(self.nc.semaphore(name))


def prepare(nc, A, G):
    with ExitStack() as ctx:
        L = Place(nc, ctx)
        ctx_sb = L.sb("ctx_sb", [KEYS, B, D])
        ctxT = L.sb("ctxT", [P, DC, B * KEYS])
        wk0 = L.sb("wk0", [P, DC, D])
        wv0 = L.sb("wv0", [P, DC, D])
        wk0r = L.sb("wk0r", [P, DC, HEADS, 8, HD])
        w1s = L.sb("w1s", [HD, 3, HD])
        w1r = L.sb("w1r", [HD, 4, 8, HD])
        gT = L.sb("gT", [P, P])
        gTm = L.sb("gTm", [P, 8, P])
        wvbd = L.sb("wvbd", [P, 8, HD])
        v0 = L.sb("v0", [KEYS, B, D])
        kf = L.sb("kf", [P, 2, B * HK])
        klo = L.sb("klo", [P, HK])
        kmid = L.sb("kmid", [P, HK])
        rw = L.sb("rw", [E, D])
        wo1 = L.sb("wo1", [P, DC, D])
        bank = [L.bank(f"prep_ps{i}") for i in range(8)]
        s_in, s_const, s_w = L.sem("p_in"), L.sem("p_const"), L.sem("p_w")
        s_pe, s_act, s_dve, s_v = L.sem("p_pe"), L.sem("p_act"), L.sem("p_dve"), L.sem("p_v")
        s_k = L.sem("p_k")
        ident = G["const"][:, CC["ident"][0]:CC["ident"][1]]
        blocks = G["const"][:, CC["blocks"][0]:CC["blocks"][1]]
        rows = G["const"][:, CC["rows"][0]:CC["rows"][1]]
        steps = []
        for b in range(B):
            steps.append(("ctxT", b))
        steps += [("rwT", 0), ("woT", 0), ("woT", 1), ("gT", 0), ("wvT", 0)]
        steps += [("v0", b) for b in range(B)] + [("v1", b) for b in range(B)]
        steps += [("k1", h) for h in range(HEADS)]
        steps += [("k0", c) for c in range(HEADS)]
        index = {s: n for n, s in enumerate(steps)}
        on_act = {("k0", c) for c in range(HEADS)} | {("k1", h) for h in range(HEADS)}
        acts = [s for s in steps if s in on_act]
        dves = [s for s in steps if s not in on_act]
        with nc.Block() as block:

            @block.sync
            def _(sp):
                sp.dma_start(G["const"][:, :], A["const"]).then_inc(s_const, 16)
                sp.dma_start(ctx_sb[:, :, :], A["ctx_1024"].rearrange("b k d -> k b d")).then_inc(s_in, 16)
                sp.dma_start(wk0[:, :, :], A["L0_xattn_Wk"].rearrange("(c p) n -> p c n", p=P)).then_inc(s_in, 16)
                sp.dma_start(wv0[:, :, :], A["L0_xattn_Wv"].rearrange("(c p) n -> p c n", p=P)).then_inc(s_in, 16)
                for n, name in enumerate(("L1_xattn_Wk", "L1_xattn_Wq", "L1_xattn_Wv")):
                    sp.dma_start(w1s[:, n, :], A[name]).then_inc(s_in, 16)
                sp.dma_start(rw[:, :], A["L0_ffn_router_w"]).then_inc(s_in, 16)
                sp.dma_start(wo1[:, :, :], A["L1_xattn_Wo"].rearrange("(c p) n -> p c n", p=P)).then_inc(s_in, 16)
                sp.dma_start(G["wq0"][:, :, :], A["L0_xattn_Wq"].rearrange("(c p) n -> p c n", p=P)).then_inc(s_w, 16)
                sp.dma_start(G["wp"][:, :, :], A["L0_xattn_Wp"].rearrange("(c p) n -> p c n", p=P)).then_inc(s_w, 16)
                sp.wait_ge(s_dve, dves.index(("v0", B - 1)) + 1)
                sp.dma_start(A["values0"].rearrange("b (k n) -> k b n", k=KEYS), v0[:, :, :]).then_inc(s_v, 16)
                sp.wait_ge(s_v, 16)
                for b in range(B):
                    sp.dma_start(G["v0"][:, b, :, 0:HD],
                                 A["values0"][b, :].rearrange("(h k n) -> k h n", h=HEADS, k=KEYS)).then_inc(s_v, 16)
                sp.wait_ge(s_v, 16 * (1 + B))
                sp.wait_ge(s_w, 32)

            @block.tensor
            def _(pe):
                mm = nc.tensor.matmul
                pe.wait_ge(s_const, 16)
                pe.wait_ge(s_in, 16 * 8)
                for n, (what, i) in enumerate(steps):
                    if n >= 8:
                        old = steps[n - 8]
                        if old in on_act:
                            pe.wait_ge(s_act, acts.index(old) + 1)
                        else:
                            pe.wait_ge(s_dve, dves.index(old) + 1)
                    ps = bank[n % 8]
                    if what == "ctxT":
                        for c in range(DC):
                            last = nc.tensor.transpose(ps[:, c * KEYS:(c + 1) * KEYS], ctx_sb[:, i, flat(c, P)],
                                                       ident[0:KEYS, 0:KEYS])
                    elif what == "rwT":
                        for c in range(DC):
                            last = nc.tensor.transpose(ps[:, c * E:(c + 1) * E], rw[:, flat(c, P)], ident[0:E, 0:E])
                    elif what == "woT":
                        for c in range(DC):
                            last = nc.tensor.transpose(ps[:, flat(c, P)], wo1[:, c, flat(i, P)], ident)
                    elif what == "gT":
                        pe.wait_ge(s_k, 1)
                        last = mm(ps[:, 0:P], w1r[:, 0, :, :].rearrange("p a b -> p (a b)"),
                                  w1r[:, 1, :, :].rearrange("p a b -> p (a b)"), start=True, stop=True)
                    elif what == "wvT":
                        last = mm(ps[:, 0:P], w1r[:, 2, :, :].rearrange("p a b -> p (a b)"),
                                  w1r[:, 3, :, :].rearrange("p a b -> p (a b)"), start=True, stop=True)
                    elif what == "v0":
                        pe.wait_ge(s_dve, dves.index(("ctxT", i)) + 1)
                        for c in range(DC):
                            last = mm(ps[0:KEYS, 0:D], ctxT[:, c, flat(i, KEYS)], wv0[:, c, :],
                                      start=c == 0, stop=c == DC - 1)
                    elif what == "v1":
                        pe.wait_ge(s_dve, dves.index(("wvT", 0)) + 1)
                        for c in range(DC):
                            last = mm(ps[0:KEYS, flat(c, P)], ctxT[:, c, flat(i, KEYS)],
                                      wvbd[:, :, :].rearrange("p a b -> p (a b)"), start=True, stop=True)
                    elif what == "k0":
                        for c in range(DC):
                            last = mm(ps[:, 0:B * KEYS], wk0r[:, c, i, :, :].rearrange("p a b -> p (a b)"),
                                      ctxT[:, c, :], start=c == 0, stop=c == DC - 1)
                    elif what == "k1":
                        last = mm(ps[:, 0:B * KEYS], gTm[:, i % 8, :], ctxT[:, i // 8, :], start=True, stop=True)
                    last.then_inc(s_pe, 1)

            @block.scalar
            def _(act):
                for m, (what, i) in enumerate(acts):
                    act.wait_ge(s_pe, index[(what, i)] + 1)
                    src = bank[index[(what, i)] % 8][:, 0:B * KEYS].rearrange("p (b k) -> p b k", b=B)
                    if what == "k0":
                        dst = kf[:, 0, :].rearrange("p (b k c) -> p b k c", b=B, c=HEADS)[:, :, :, i]
                    else:
                        dst = kf[:, 1, :].rearrange("p (b h k) -> p b h k", b=B, h=HEADS)[:, :, i, :]
                    nc.scalar.activation(dst, src, ACT.Copy).then_inc(s_act, 1)

            @block.vector
            def _(dve):
                dve.wait_ge(s_in, 16 * 8)
                dve.wait_ge(s_const, 16)
                for n in range(3):
                    nc.vector.tensor_copy(w1r[:, n, :, :], w1s[:, n, :][:, None, :].broadcast_to([HD, 8, HD]))
                nc.vector.tensor_copy(w1r[:, 3, :, :], ident[0:HD, 0:HD][:, None, :].broadcast_to([HD, 8, HD]))
                for c in range(DC):
                    last = nc.vector.tensor_copy(
                        wk0r[:, c, :, :, :],
                        wk0[:, c, :].rearrange("p (h e) -> p h e", h=HEADS)[:, :, None, :].broadcast_to([P, HEADS, 8, HD]))
                last.then_inc(s_k, 1)
                nc.vector.memset(G["v0"][:, :, :, HD:VW], 1.0)
                nc.vector.memset(G["v1"][:, :, :, HD:VW], 1.0)
                nc.vector.tensor_copy(G["ident16"][:, :], ident)
                nc.vector.tensor_copy(G["tri16"][:, :], G["const"][:, CC["tri"][0]:CC["tri"][1]])
                nc.vector.memset(G["ones16"][:, :], 1.0)
                nc.vector.tensor_copy(G["early"][:, :], G["const"][0:5, CC["early"][0]:CC["early"][1]])
                nc.vector.tensor_copy(G["late"][:, :], G["const"][0:5, CC["latekeys"][0]:CC["latekeys"][1]])
                nc.vector.tensor_copy(G["blocks16"][:, :], blocks)
                nc.vector.memset(G["neghalf"][:, :], -0.5)
                for what, i in dves:
                    dve.wait_ge(s_pe, index[(what, i)] + 1)
                    ps = bank[index[(what, i)] % 8]
                    if what == "ctxT":
                        last = nc.vector.tensor_copy(ctxT[:, :, flat(i, KEYS)],
                                                     ps[:, 0:DC * KEYS].rearrange("p (c k) -> p c k", c=DC))
                    elif what == "rwT":
                        last = nc.vector.tensor_copy(G["rwT"][:, :, :], ps[:, 0:DC * E].rearrange("p (c k) -> p c k", c=DC))
                    elif what == "woT":
                        last = nc.vector.tensor_copy(G["woT"][:, i, :], ps[:, 0:D])
                    elif what == "gT":
                        for m in range(8):
                            last = nc.vector.tensor_scalar(gTm[:, m, :], ps[:, 0:P], blocks[:, m:m + 1], None, ALU.mult)
                    elif what == "wvT":
                        last = nc.vector.tensor_tensor(wvbd[:, :, :], ps[:, 0:P].rearrange("p (a b) -> p a b", a=8),
                                                       blocks[:, :, None].broadcast_to([P, 8, HD]), ALU.mult)
                    elif what == "v0":
                        last = nc.vector.tensor_copy(v0[:, i, :], ps[0:KEYS, 0:D])
                    elif what == "v1":
                        last = nc.vector.tensor_copy(G["v1"][:, i, :, 0:HD],
                                                     ps[0:KEYS, 0:D].rearrange("p (h e) -> p h e", h=HEADS))
                    last.then_inc(s_dve, 1)
                for n, layer in enumerate((1, 0)):
                    dve.wait_ge(s_act, HEADS * (n + 1))
                    for b in range(B):
                        k = 1 + 3 * (B * n + b)
                        hi = G["khi"][layer][:, b, :]
                        src = kf[:, layer, flat(b, HK)]
                        nc.vector.tensor_copy(hi, src).then_inc(s_k, 1)
                        dve.wait_ge(s_k, k + 1)
                        nc.vector.tensor_tensor(klo[:, :], src, hi, ALU.subtract).then_inc(s_k, 1)
                        dve.wait_ge(s_k, k + 2)
                        nc.vector.tensor_scalar(kmid[:, :], klo[:, :], rows[:, 1:2], rows[:, 2:3], ALU.mult, ALU.add) \
                            .then_inc(s_k, 1)
                        dve.wait_ge(s_k, k + 3)
                        nc.vector.scalar_tensor_tensor(G["kcat"][layer][:, b, :], hi, rows[:, 0:1], kmid[:, :],
                                                       ALU.mult, ALU.add)


def attention(nc, A, G, layer):
    first = layer == 0
    with ExitStack() as ctx:
        L = Place(nc, ctx)
        x = L.sb(f"x{layer}", [P, 4, D])
        stats = L.sb(f"stats{layer}", [P, 4, 6])
        mv = L.sb(f"mv{layer}", [P, 4, 2])
        ve = L.sb(f"ve{layer}", [P, 4, 1])
        rstd = L.sb(f"rstd{layer}", [P, 4, 1])
        xh = L.sb(f"xh{layer}", [P, 4, D])
        xhT = L.sb(f"xhT{layer}", [P, 2, D])
        qcat = L.sb(f"qcat{layer}", [P, 4, HEADS, HR], F16)
        qhi = L.sb(f"qhi{layer}", [P, 4, D], F16)
        qhT = L.sb(f"qhT{layer}", [P, 2, DC, P], F16)
        nmax = L.sb(f"nmax{layer}", [P, 2, HEADS])
        bd = L.sb(f"bd{layer}", [P, 2, 2, 8, KEYS], F16)
        kcat = L.sb(f"kcat_u{layer}", [P, 2, HK], F16)
        vhi = L.sb(f"vhi{layer}", [KEYS, 2, HEADS, VW], F16)
        vlo = L.sb(f"vlo{layer}", [KEYS, 2, HEADS, VW], F16)
        qT = L.sb(f"qT{layer}", [P, 2, 8, P], F16)
        pT = L.sb(f"pT{layer}", [KEYS, HEADS * P])
        phi = L.sb(f"phi{layer}", [KEYS, 2, 8 * S], F16)
        plo = L.sb(f"plo{layer}", [KEYS, 2, 8 * S], F16)
        rec = L.sb(f"rec{layer}", [P, 2, HEADS])
        o = L.sb(f"o{layer}", [P, 2, HEADS, HD])
        y1 = y2 = None
        if not first:
            y1 = L.sb("y1", [P, 4, D])
            y2 = L.sb("y2", [P, 4, D])
            xa = L.sb("xa", [P, 2, D])
            x2 = L.sb("x2", [P, 4, D])
            slots = L.sb("slots", [P, 4, 2], I32)
        tr_ps = L.bank(f"tr_ps{layer}")
        qh_ps = tr_ps[:, 0:P].bitcast(F16)
        q_ps = L.bank(f"q_ps{layer}")
        s_ps = [L.bank(f"s_ps{layer}_{i}") for i in range(2)]
        qT_ps = L.bank(f"qT_ps{layer}", F16)
        sT_ps = [L.bank(f"sT_ps{layer}_{i}") for i in range(2)]
        o_ps = L.bank(f"o_ps{layer}")
        sem = lambda n: L.sem(f"{n}_{layer}")
        x_in = [sem(f"x_in{i}") for i in range(4)]
        y_in = [sem(f"y_in{i}") for i in range(4)] if not first else None
        var_ok, rstd_ok, xh_ok, norm_ch = sem("var_ok"), sem("rstd_ok"), sem("xh_ok"), sem("norm_ch")
        qhi_ok, qlo_ok = sem("qhi_ok"), sem("qlo_ok")
        if first:
            xhT_ps, xhT_ok, q_done, mask_ok = (sem(n) for n in ("xhT_ps", "xhT_ok", "q_done", "mask_ok"))
        qhT_ps, qhT_ok, bd_ok, s_done, max_ok, m_ok, m_ch = (
            sem(n) for n in ("qhT_ps", "qhT_ok", "bd_ok", "s_done", "max_ok", "m_ok", "m_ch"))
        kcat_ok, vu_ok, qT_done, qT_ok, sT_done, exp_ok = (
            sem(n) for n in ("kcat_ok", "vu_ok", "qT_done", "qT_ok", "sT_done", "exp_ok"))
        o_done, rec_ok, o_ok, phi_ok, plo_ok = (sem(n) for n in ("o_done", "rec_ok", "o_ok", "phi_ok", "plo_ok"))
        o_out = [sem(f"o_out{i}") for i in range(2)]
        if not first:
            slots_ok, x2_ok, x2_out = sem("slots_ok"), sem("x2_ok"), [sem(f"x2_out{i}") for i in range(4)]
        ident = G["const"][:, CC["ident"][0]:CC["ident"][1]]
        seen = G["const"][0:KEYS, CC["seen"][0]:CC["seen"][1]].rearrange("p (c t) -> p c t", t=5)
        OUTS = 4 if first else 1
        AHEAD = 16

        def batches(eng, step, ahead=False):
            def body(bb, lo, hi, end):
                for s in range(TB):
                    step(bb, s, lambda k: lo <= s - k < (hi if k >= 0 else end))
            body(0, 0, TB, TB + 1)
            with eng.Fori(1, B - 1 if ahead else B) as bb:
                body(bb, -TB, TB, TB + 1)
            if ahead:
                body(B - 1, -TB, TB, TB)
            body(B, -TB, 0, 0)

        def count(bb, s, back, per=1, plus=0):
            return bb * (TB * per) + ((s - back) * per + plus)

        def times4(bb, s, back, per=16):
            return bb * (2 * per) + ((s - back) // 4 + 1) * per

        def times2(bb, s, back, per):
            return bb * (4 * per) + ((s - back) // 2 + 1) * per

        def part(s, back, half):
            k = (s - back) % TB
            return (slice(None), k // 4, ds(k % 4 * (HEADS * P) + half * 1024, 1024)), pT[:, flat(half, 1024)]

        src_x = A["x"].rearrange("b s d -> (b s) d") if first else A["x1"]
        with nc.Block() as block:

            @block.sync
            def _(sp):
                for k in range(2):
                    sp.sem_inc(o_out[k], AHEAD)

                def load(bb, s):
                    after(sp, xh_ok if first else x2_ok, count(bb, s, 4, 1, 1))
                    sp.dma_start(x[:, s % 4, :], src_x[ds(bb * S + s * P, P), :]).then_inc(x_in[s % 4], 16)

                load(0, 0)

                def step(bb, s, live):
                    if live(-1):
                        load(bb, s + 1)
                    if not first and live(2):
                        k = (s - 2) % 4
                        sp.wait_ge(x2_ok, count(bb, s, 2, 1, 1))
                        sp.dma_start(A["x2"][ds(bb * S + (s - 2) * P, P), :], x2[:, k, :]).then_inc(x2_out[k], 16)
                    if live(8):
                        k, u = s % 2, s // 4
                        sp.wait_ge(o_ok, count(bb, s, 8, 1, 1) + AHEAD)
                        if first:
                            for n in range(2):
                                st = 2 * (s % 4) + n
                                r, q = st // 4, st % 4
                                for jp in range(2):
                                    dst = A["attn"].rearrange("(b t q j r) d -> b q j r t d", b=B, q=4, j=2, r=2)
                                    sp.dma_start(dst[ds(bb - 1, 1), q, jp, r, :, flat(u, P)],
                                                 o[flat(jp, 64), k, flat(n, 8), :].rearrange("p h e -> p (h e)")) \
                                        .then_inc(o_out[k], 16)
                        else:
                            sp.dma_start(A["attn1"][ds(bb * S + (s - 8) * P, P), :],
                                         o[:, k, :, :].rearrange("p h e -> p (h e)")).then_inc(o_out[k], 16)
                batches(sp, step, ahead=True)
                for k in range(2):
                    sp.wait_ge(o_out[k], 16 * OUTS * NT // 2 + AHEAD)
                if not first:
                    for k in range(4):
                        sp.wait_ge(x2_out[k], 16 * NT // 4)

            @block.gpsimd
            def _(pool):
                def gather(bb, s):
                        after(pool, x2_ok, count(bb, s, 4, 1, 1))
                        bs, ss = (bb, s) if s < TB else (bb + 1, s - TB)
                        nc.gpsimd.tensor_copy(slots[:, s % 4, :], G["slots_t"][:, ss, :, ds(bs, 1)]).then_inc(slots_ok, 1)
                        apart(pool, slots_ok, count(bb, s, 0, 1, 1), G["pool_passed"])
                        for n, y in enumerate((y1, y2)):
                            pool.indirect_dma_start(
                                out=y[:, s % 4, :], out_offset=None, in_=A["y"],
                                in_offset=bass.IndirectOffsetOnAxis(ap=slots[:, s % 4, n:n + 1], axis=0)) \
                                .then_inc(y_in[s % 4], 16)

                if not first:
                    gather(0, 0)

                def step(bb, s, live):
                    h = s // 4
                    if not first and live(-1):
                        gather(bb, s + 1)
                    if first and live(2) or not first and live(0) and s % 4 == 0:
                        k = s - 2 if first else s
                        u = k // 4
                        ring = k % 2 if first else h
                        for n in range(2):
                            if first:
                                base = bb * HK + ((2 * k + n) * KEYS if k >= 0 else (2 * (k + TB) + n) * KEYS - HK)
                                if n == 0 and live(4):
                                    apart(pool, s_done, count(bb, s, 4, 4, 4), G["pool_passed"])
                                src = G["khi"][0][:, :, :].rearrange("p b f -> p (b f)")[:, None, ds(base, KEYS)] \
                                    .broadcast_to([P, 8, KEYS])
                            else:
                                if n == 0 and live(5):
                                    apart(pool, s_done, count(bb, s, 5, 4, 4), G["pool_passed"])
                                src = G["khi"][1][:, :, :].rearrange("p b f -> p (b f)")[
                                    :, ds(bb * HK + n * 8 * KEYS, 8 * KEYS)].rearrange("p (j k) -> p j k", j=8)
                            nc.gpsimd.tensor_tensor(bd[:, ring, n, :, :], src,
                                                    G["blocks16"][:, :, None].broadcast_to([P, 8, KEYS]), ALU.mult) \
                                .then_inc(bd_ok, 1)
                    if live(0):
                        pool.wait_ge(var_ok, count(bb, s, 0, 1, 1))
                        nc.gpsimd.tensor_tensor(rstd[:, s % 4, :], ve[:, s % 4, :], G["neghalf"][:, :], ALU.pow) \
                            .then_inc(rstd_ok, 1)
                batches(pool, step, ahead=not first)

            @block.tensor
            def _(pe):
                mm = nc.tensor.matmul
                pe.sem_inc(o_done, AHEAD)

                def high_transposed(bb, s, live):
                    k = (s - 2) % 4
                    pe.wait_ge(qhi_ok, count(bb, s, 2, 1, 1))
                    if first:
                        pe.wait_ge(xhT_ok, count(bb, s, 1, 1, 1 if live(1) else 0))
                    else:
                        after(pe, qhT_ok, count(bb, s, 3, 1, 1))
                    for c in range(DC):
                        last = nc.tensor.transpose(qh_ps[:, flat(c, P)], qhi[:, k, flat(c, P)], G["ident16"][:, :])
                    last.then_inc(qhT_ps, 1)

                def queries(bb, s):
                    k = (s - 1) % 2
                    pe.wait_ge(xhT_ok, count(bb, s, 1, 1, 1))
                    after(pe, qlo_ok, count(bb, s, 2, 1, 1))
                    for c in range(DC):
                        last = mm(q_ps[:, 0:D], xhT[:, k, flat(c, P)], G["wq0"][:, c, :], start=c == 0, stop=c == DC - 1)
                    last.then_inc(q_done, 1)

                def rows_transposed(bb, s, live):
                    pe.wait_ge(xh_ok, count(bb, s, 0, 1, 1))
                    if live(2):
                        pe.wait_ge(qhT_ok, count(bb, s, 2, 1, 1))
                    else:
                        after(pe, xhT_ok, count(bb, s, 1, 1, 1))
                    for c in range(DC):
                        last = nc.tensor.transpose(tr_ps[:, flat(c, P)], xh[:, s % 4, flat(c, P)], ident)
                    last.then_inc(xhT_ps, 1)

                def scores(bb, s, g):
                    k = (s - 2) % 2
                    if g == 0:
                        pe.wait_ge(qhT_ok, count(bb, s, 2, 1, 1))
                        if first:
                            pe.wait_ge(bd_ok, count(bb, s, 2, 2, 2))
                        else:
                            pe.wait_ge(bd_ok, bb * 4 + ((s - 2) // 4 + 1) * 2)
                    ps = s_ps[g % 2][:, 0:CH]
                    after(pe, max_ok, count(bb, s, 2, 4, g - 1))
                    cols = slice(g % 2 * 4, g % 2 * 4 + 4)
                    if first:
                        for n in range(2):
                            mm(ps[flat(n, 64), :], qhT[:, k, g // 2, flat(n, 64)],
                               bd[:, k, n, cols, :].rearrange("p j k -> p (j k)"), start=True, stop=False)
                        last = mm(ps, G["early"][:, :], G["late"][:, flat(g, CH)], start=False, stop=True)
                    else:
                        last = mm(ps, qhT[:, k, g // 2, :],
                                  bd[:, (s - 2) % TB // 4, g // 2, cols, :].rearrange("p j k -> p (j k)"),
                                  start=True, stop=True)
                    last.then_inc(s_done, 1)

                def all_transposed(bb, s):
                    k = (s - 3) % 4
                    pe.wait_ge(m_ok, count(bb, s, 3, 1, 1))
                    pe.wait_ge(qlo_ok, count(bb, s, 3, 1, 1))
                    after(pe, qT_ok, count(bb, s, 4, 1, 1))
                    for j in range(8):
                        last = nc.tensor.transpose(qT_ps[:, flat(j, P)],
                                                   qcat[:, k, 2 * j:2 * j + 2, :].rearrange("p a b -> p (a b)"),
                                                   G["ident16"][:, :])
                    last.then_inc(qT_done, 1)

                def scores_by_key(bb, s, g):
                    k, h = (s - 4) % TB, (s - 4) % TB // 4
                    if g == 0:
                        pe.wait_ge(qT_ok, count(bb, s, 4, 1, 1))
                        pe.wait_ge(kcat_ok, bb * 2 + ((s - 4) // 4 + 1))
                    ps = sT_ps[g % 2][0:KEYS, :]
                    after(pe, exp_ok, count(bb, s, 4, 4, g - 1))
                    r = g % 2
                    if first:
                        n = g // 2
                        last = mm(ps, kcat[flat(r, HR), h, flat(2 * k + n, KEYS)],
                                  qT[flat(r, HR), k % 2, :, flat(n, 64)], start=True, stop=True)
                    else:
                        for i in range(4):
                            jj = g // 2 * 4 + i
                            last = mm(ps[:, flat(i, P)], kcat[flat(r, HR), h, flat(2 * jj + r, KEYS)],
                                      qT[flat(r, HR), k % 2, jj, :], start=True, stop=True)
                    last.then_inc(sT_done, 1)

                def values(bb, s, part):
                    u = s // 4
                    if part == 0:
                        pe.wait_ge(vu_ok, bb * 4 + (u - 1) * 2)
                        if first:
                            pe.wait_ge(plo_ok, bb * (2 * TB) + (u * 4 - 4) * 2)
                        else:
                            pe.wait_ge(plo_ok, count(bb, s, 8, 2, 2))
                        pe.wait_ge(o_ok, count(bb, s, 9, 1, 1) + AHEAD)
                    for m in range(part * 4, part * 4 + 4):
                        n, hl = m // 8, m % 8
                        if first:
                            st = 2 * (s % 4) + n
                            at, head = hl * S + st * P, u * 8 + hl
                        else:
                            place = m // 8 * 8 + m % 2 * 4 + m // 2 % 4
                            at, head = s % 4 * (HEADS * P) + place * P, m
                        out = o_ps[:, ds(m * VW, VW)]
                        mm(out, phi[:, u, ds(at, P)], vhi[:, u, head, :], start=True, stop=False)
                        mm(out, phi[:, u, ds(at, P)], vlo[:, u, head, :], start=False, stop=False)
                        last = mm(out, plo[:, u, ds(at, P)], vhi[:, u, head, :], start=False, stop=True)
                    if part == 3:
                        last.then_inc(o_done, 1)

                def step(bb, s, live):
                    if live(2):
                        high_transposed(bb, s, live)
                    if live(4):
                        scores_by_key(bb, s, 0)
                        scores_by_key(bb, s, 1)
                    if live(3):
                        all_transposed(bb, s)
                    if first and live(1):
                        queries(bb, s)
                    for g in range(4):
                        if live(2):
                            scores(bb, s, g)
                        if live(4) and g in (1, 2):
                            scores_by_key(bb, s, g + 1)
                        if live(8):
                            values(bb, s, g)
                    if first and live(0):
                        rows_transposed(bb, s, live)
                batches(pe, step)

            @block.scalar
            def _(act):
                def exps(bb, s, g):
                    if g % 2 == 0:
                        after(act, plo_ok, count(bb, s, 5, 2, g // 2 + 1))
                    act.wait_ge(sT_done, count(bb, s, 4, 4, g + 1))
                    nc.scalar.activation(pT[:, flat(g, 512)], sT_ps[g % 2][0:KEYS, :], ACT.Exp,
                                         scale=1.0 if first else 1.0 / 16).then_inc(exp_ok, 1)

                def high(bb, s, back, half):
                    if half == 0 and not (isinstance(bb, int) and bb * TB + s < 12):
                        act.wait_ge(o_done, bb * TB + ((s - 4) // 4 * 4 - 4) + AHEAD)
                    if first:
                        act.wait_ge(mask_ok, count(bb, s, back, 2, half + 1))
                    else:
                        act.wait_ge(exp_ok, count(bb, s, back, 4, 2 * half + 2))
                    place, probs = part(s, back, half)
                    nc.scalar.activation(phi[place], probs, ACT.Copy).then_inc(phi_ok, 1)

                def step(bb, s, live):
                    if live(5):
                        high(bb, s, 5, 1)
                    if live(4):
                        exps(bb, s, 0)
                        exps(bb, s, 1)
                    if live(1):
                        k = (s - 1) % 4
                        if first:
                            act.wait_ge(q_done, count(bb, s, 1, 1, 1))
                            src = q_ps[:, 0:D]
                        else:
                            act.wait_ge(xh_ok, count(bb, s, 1, 1, 1))
                            src = xh[:, k, :]
                        after(act, qT_done, count(bb, s, 5, 1, 1))
                        nc.scalar.activation(qhi[:, k, :], src, ACT.Copy).then_inc(qhi_ok, 1)
                    if live(3):
                        k = (s - 3) % 2
                        act.wait_ge(qT_done, count(bb, s, 3, 1, 1))
                        after(act, sT_done, count(bb, s, 5, 4, 4))
                        nc.scalar.activation(qT[:, k, :, :], qT_ps[:, :].rearrange("p (j t) -> p j t", j=8),
                                             ACT.Copy).then_inc(qT_ok, 1)
                    if live(4):
                        exps(bb, s, 2)
                        exps(bb, s, 3)
                        high(bb, s, 4, 0)
                    if first and live(0):
                        act.wait_ge(xhT_ps, count(bb, s, 0, 1, 1))
                        after(act, q_done, count(bb, s, 2, 1, 1))
                        nc.scalar.activation(xhT[:, s % 2, :], tr_ps[:, 0:D], ACT.Copy).then_inc(xhT_ok, 1)
                batches(act, step)

            @block.vector
            def _(dve):
                nc.vector.memset(qcat[:, :, :, :], 0.0)
                dve.sem_inc(o_ok, AHEAD)

                def residual(bb, s):
                    k = s % 4
                    dve.wait_ge(y_in[k], times4(bb, s, 0, 32))
                    dve.wait_ge(x_in[k], times4(bb, s, 0, 16))
                    after(dve, x2_out[k], times4(bb, s, 4, 16))
                    nc.vector.scalar_tensor_tensor(xa[:, s % 2, :], y1[:, k, :], G["cw_t"][:, s, 0, ds(bb, 1)],
                                                   x[:, k, :], ALU.mult, ALU.add).then_inc(norm_ch, 1)
                    dve.wait_ge(norm_ch, count(bb, s, 0, 3, 1))
                    nc.vector.scalar_tensor_tensor(x2[:, k, :], y2[:, k, :], G["cw_t"][:, s, 1, ds(bb, 1)],
                                                   xa[:, s % 2, :], ALU.mult, ALU.add).then_inc(x2_ok, 1)
                    dve.wait_ge(x2_ok, count(bb, s, 0, 1, 1))

                def low(bb, s, back, half):
                    place, probs = part(s, back, half)
                    dve.wait_ge(phi_ok, count(bb, s, back, 2, half + 1))
                    nc.vector.tensor_tensor(plo[place], probs, phi[place], ALU.subtract).then_inc(plo_ok, 1)

                def mask(bb, s, n):
                    dve.wait_ge(exp_ok, count(bb, s, 4, 4, 2 * n + 2))
                    early = pT[:, flat(n, S)].rearrange("p (c t) -> p c t", t=64)[:, :, 0:5]
                    nc.vector.scalar_tensor_tensor(early, early, 3e38, seen, ALU.min, ALU.mult).then_inc(mask_ok, 1)

                def maximum(bb, s, g):
                    dve.wait_ge(s_done, count(bb, s, 2, 4, g + 1))
                    nc.vector.tensor_reduce(nmax[:, s % 2, 4 * g:4 * g + 4],
                                            s_ps[g % 2][:, 0:CH].rearrange("p (j k) -> p j k", j=4),
                                            AX.X, ALU.max, negate=True).then_inc(max_ok, 1)

                def step(bb, s, live):
                    if s % 4 == 0 and live(0):
                        after(dve, sT_done, count(bb, s, 4, 4, 0))
                        n0, n1 = ((s // 4) * 8 * KEYS, 8 * KEYS) if first else (0, HK)
                        nc.vector.tensor_scalar(kcat[:, s // 4, ds(n0, n1)],
                                                G["kcat"][layer][:, :, :].rearrange("p b f -> p (b f)")[:, ds(bb * HK + n0, n1)],
                                                1.0, None, ALU.mult) \
                            .then_inc(kcat_ok, 1)
                    if live(2):
                        dve.wait_ge(qhT_ps, count(bb, s, 2, 1, 1))
                        after(dve, s_done, count(bb, s, 4, 4, 4))
                        nc.vector.tensor_copy(qhT[:, (s - 2) % 2, :, :], qh_ps[:, 0:D].rearrange("p (c t) -> p c t", c=DC)) \
                            .then_inc(qhT_ok, 1)
                    if live(0):
                        k = s % 4
                        if first:
                            dve.wait_ge(x_in[k], times4(bb, s, 0, 16))
                            xin, per = x, 2
                        else:
                            residual(bb, s)
                            xin, per = x2, 3
                        nc.vector.bn_stats(stats[:, k, :], xin[:, k, :]).then_inc(norm_ch, 1)
                        apart(dve, norm_ch, count(bb, s, 0, per, per - 1), G["dve_passed"])
                        nc.vector.bn_aggr(mv[:, k, :], stats[:, k, :]).then_inc(norm_ch, 1)
                        dve.wait_ge(norm_ch, count(bb, s, 0, per, per))
                        nc.vector.tensor_scalar(ve[:, k, :], mv[:, k, 1:2], EPS, None, ALU.add).then_inc(var_ok, 1)
                    if live(5):
                        low(bb, s, 5, 1)
                    if live(2):
                        maximum(bb, s, 0)
                    if live(1):
                        k = (s - 1) % 4
                        src = q_ps[:, 0:D] if first else xh[:, k, :]
                        dve.wait_ge(qhi_ok, count(bb, s, 1, 1, 1))
                        hi = qhi[:, k, :].rearrange("p (h e) -> p h e", h=HEADS)
                        nc.vector.tensor_copy(qcat[:, k, :, 0:HD], hi)
                        nc.vector.tensor_copy(qcat[:, k, :, 2 * HD:3 * HD], hi)
                        nc.vector.tensor_tensor(qcat[:, k, :, HD:2 * HD], src.rearrange("p (h e) -> p h e", h=HEADS),
                                                hi, ALU.subtract).then_inc(qlo_ok, 1)
                    if live(2):
                        maximum(bb, s, 1)
                    if first and live(4):
                        mask(bb, s, 0)
                    if live(0):
                        k = s % 4
                        dve.wait_ge(rstd_ok, count(bb, s, 0, 1, 1))
                        if first:
                            after(dve, xhT_ps, count(bb, s, 4, 1, 1))
                        else:
                            after(dve, qlo_ok, count(bb, s, 4, 1, 1))
                        nc.vector.tensor_scalar(xh[:, k, :], (x if first else x2)[:, k, :], mv[:, k, 0:1],
                                                rstd[:, k, :], ALU.subtract, ALU.mult).then_inc(xh_ok, 1)
                    if live(2):
                        maximum(bb, s, 2)
                        maximum(bb, s, 3)
                        q4 = qcat[:, (s - 2) % 4, :, :]
                        dve.wait_ge(max_ok, count(bb, s, 2, 4, 4))
                        nc.vector.tensor_scalar(q4[:, :, 3 * HD], nmax[:, s % 2, :], 1 / MSCALE, None, ALU.mult).then_inc(m_ch, 1)
                        dve.wait_ge(m_ch, count(bb, s, 2, 1, 1))
                        nc.vector.scalar_tensor_tensor(q4[:, :, 3 * HD + 1], nmax[:, s % 2, :], 1 / MSCALE, q4[:, :, 3 * HD],
                                                       ALU.mult, ALU.subtract).then_inc(m_ok, 1)
                    if live(4):
                        if first:
                            mask(bb, s, 1)
                        low(bb, s, 4, 0)
                    if live(8):
                        dve.wait_ge(o_done, count(bb, s, 8, 1, 1) + AHEAD)
                        k = s % 2
                        ov = o_ps[:, 0:HEADS * VW].rearrange("p (h e) -> p h e", h=HEADS)
                        if not (isinstance(bb, int) and bb * TB + s < 10):
                            dve.wait_ge(o_out[k], times2(bb, s, 10, 16 * OUTS) + AHEAD)
                        nc.vector.reciprocal(rec[:, k, :], ov[:, :, HD]).then_inc(rec_ok, 1)
                        dve.wait_ge(rec_ok, count(bb, s, 8, 1, 1))
                        nc.vector.tensor_tensor(o[:, k, :, :], ov[:, :, 0:HD],
                                                rec[:, k, :, None].broadcast_to([P, HEADS, HD]), ALU.mult).then_inc(o_ok, 1)
                    if s % 4 == 3 and live(7):
                        if not (isinstance(bb, int) and bb * TB + s < 11):
                            dve.wait_ge(o_done, bb * TB + (s - 11) + AHEAD)
                        src = (G["v0"] if first else G["v1"])[:, ds(bb if s >= 7 else bb - 1, 1), :, :] \
                            .rearrange("p o h e -> p (o h) e")
                        half = (s - 7) % TB // 4
                        nc.vector.tensor_scalar(vhi[:, half, :, :], src, 1.0, None, ALU.mult).then_inc(vu_ok, 1)
                        dve.wait_ge(vu_ok, bb * 4 + ((s - 7) // 4 * 2 + 1))
                        nc.vector.scalar_tensor_tensor(vlo[:, half, :, :], src, 1.0, vhi[:, half, :, :],
                                                       ALU.mult, ALU.subtract).then_inc(vu_ok, 1)
                batches(dve, step)


def allocate(nc, ctx):
    L = Place(nc, ctx)
    return {
        "dve_passed": L.sem("dve_passed"), "pool_passed": L.sem("pool_passed"),
        "const": L.sb("const", [P, CW]), "ident16": L.sb("ident16", [P, P], F16), "tri16": L.sb("tri16", [P, P], F16),
        "ones16": L.sb("ones16", [P, P], F16), "blocks16": L.sb("blocks16", [P, 8], F16),
        "neghalf": L.sb("neghalf", [P, 1]), "rwT": L.sb("rwT", [P, DC, E]),
        "woT": L.sb("woT", [P, DC, D]), "wp": L.sb("wp", [P, DC, D]),
        "v1": L.sb("v1_sb", [KEYS, B, HEADS, VW]),
        "logits": L.sb("logits", [P, NT, E]), "cw_t": L.sb("cw_t", [P, TB, 2, B]),
        "slots_t": L.sb("slots_t", [P, TB, 2, B], I32), "token": L.sb("token", [P, HALFT], I32),
        "tile_expert": L.sb("tile_expert", [1, ET], I32),
        "khi": [None, L.sb("khi1", [P, B, HK], F16)], "kcat": [None, L.sb("kcat1", [P, B, HK], F16)],
    }


def allocate_first(nc, ctx, G):
    L = Place(nc, ctx)
    G["early"], G["late"] = L.sb("early", [5, P], BF16), L.sb("late", [5, HEADS * KEYS], BF16)
    G["wq0"], G["v0"] = L.sb("wq0", [P, DC, D]), L.sb("v0_sb", [KEYS, B, HEADS, VW])
    G["khi"][0], G["kcat"][0] = L.sb("khi0", [P, B, HK], F16), L.sb("kcat0", [P, B, HK], F16)


def normed(nc, dve, xin, stats, mv, ve, sem, at, var_ok, passed):
    nc.vector.bn_stats(stats, xin).then_inc(sem, 1)
    apart(dve, sem, at + 1, passed)
    nc.vector.bn_aggr(mv, stats).then_inc(sem, 1)
    dve.wait_ge(sem, at + 2)
    nc.vector.tensor_scalar(ve, mv[:, 1:2], EPS, None, ALU.add).then_inc(var_ok, 1)


def project(nc, A, G):
    RING = 4
    with ExitStack() as ctx:
        L = Place(nc, ctx)
        at = L.sb("at_p", [P, RING, D])
        x = L.sb("x_p", [P, RING, D])
        w = L.sb("w_p", [P, RING, HID])
        atT = L.sb("atT_p", [P, 2, D])
        x1 = L.sb("x1_p", [P, RING, D])
        xh = L.sb("xh_p", [P, RING, D])
        xhT = L.sb("xhT_p", [P, 2, D])
        stats, mv = L.sb("stats_p", [P, RING, 6]), L.sb("mv_p", [P, RING, 2])
        ve, rstd = L.sb("ve_p", [P, RING, 1]), L.sb("rstd_p", [P, RING, 1])
        at_ps, pr_ps, xh_ps, lg_ps = (L.bank(f"{n}_ps_p") for n in ("at", "pr", "xh", "lg"))
        ax_in = [L.sem(f"ax_in{i}") for i in range(RING)]
        w_in = [L.sem(f"w_in{i}") for i in range(RING)]
        x1_out = [L.sem(f"x1_out{i}") for i in range(RING)]
        at_done, atT_ok, pr_done, x1_ok, ch, var_ok, rstd_ok, xh_ok = (
            L.sem(f"{n}_p") for n in ("at_done", "atT_ok", "pr_done", "x1_ok", "ch", "var_ok", "rstd_ok", "xh_ok"))
        xh_done, xhT_ok, lg_done, lg_ok, whi_ok, wlo_ok = (
            L.sem(f"{n}_p") for n in ("xh_done", "xhT_ok", "lg_done", "lg_ok", "whi_ok", "wlo_ok"))
        ident = G["const"][:, CC["ident"][0]:CC["ident"][1]]
        GROUPS = NT // RING

        AHEAD = 16

        def groups(eng, step, ahead=False):
            def body(g, lo, hi, end):
                for s in range(RING):
                    step(g, s, lambda k: lo <= s - k < (hi if k >= 0 else end))
            body(0, 0, RING, RING + 1)
            with eng.Fori(1, GROUPS - 1 if ahead else GROUPS) as g:
                body(g, -RING, RING, RING + 1)
            if ahead:
                body(GROUPS - 1, -RING, RING, RING)
            body(GROUPS, -RING, 0, 0)

        def upto(g, s, back, per=1, plus=1):
            return g * (RING * per) + ((s - back) * per + plus)

        def slot(g, s, back, per=16):
            return g * per + ((s - back) // RING + 1) * per

        with nc.Block() as block:

            @block.sync
            def _(sp):
                for k in range(RING):
                    sp.sem_inc(x1_out[k], AHEAD)

                def load(g, s):
                    row = ds(g * (RING * P) + s * P, P)
                    k, e = s % RING, s // RING
                    after(sp, x1_ok, upto(g, s, 4))
                    sp.dma_start(at[:, k, :], A["attn"][row, :]).then_inc(ax_in[k], 16)
                    sp.dma_start(x[:, k, :], A["x"].rearrange("b s d -> (b s) d")[row, :]).then_inc(ax_in[k], 16)
                    after(sp, wlo_ok, upto(g, s, 4))
                    if k < DC:
                        src = A["L0_ffn_w1"].rearrange("e r n -> (e r) n")[ds(g * D + (e * D + k * P), P), :]
                        dst = w[:, k, :]
                    else:
                        src = A["L0_ffn_w2"].rearrange("e r d -> (e r) d")[ds(g * HID + (e * HID + (k - DC) * (HID // 2)), HID // 2), :] \
                            .rearrange("(m p) d -> p m d", p=P)
                        dst = w[:, k, :].rearrange("p (m d) -> p m d", d=D)
                    sp.dma_start(dst, src).then_inc(w_in[k], 16)

                load(0, 0)

                def step(g, s, live):
                    if live(-1):
                        load(g, s + 1)
                    if live(2):
                        k = (s - 2) % RING
                        row = ds(g * (RING * P) + (s - 2) * P, P)
                        sp.wait_ge(x1_ok, upto(g, s, 2))
                        sp.dma_start(A["x1"][row, :], x1[:, k, :]).then_inc(x1_out[k], 16)
                        sp.wait_ge(xh_ok, upto(g, s, 2))
                        sp.dma_start(A["xh"][row, :], xh[:, k, :]).then_inc(x1_out[k], 16)
                groups(sp, step, ahead=True)
                for k in range(RING):
                    sp.wait_ge(x1_out[k], 32 * GROUPS + AHEAD)

            @block.gpsimd
            def _(pool):
                def step(g, s, live):
                    if live(1):
                        k = (s - 1) % RING
                        pool.wait_ge(var_ok, upto(g, s, 1))
                        nc.gpsimd.tensor_tensor(rstd[:, k, :], ve[:, k, :], G["neghalf"][:, :], ALU.pow).then_inc(rstd_ok, 1)
                groups(pool, step)

            @block.tensor
            def _(pe):
                mm = nc.tensor.matmul
                def step(g, s, live):
                    if live(1):
                        pe.wait_ge(atT_ok, upto(g, s, 1))
                        after(pe, x1_ok, upto(g, s, 2))
                        for c in range(DC):
                            last = mm(pr_ps[:, 0:D], atT[:, (s - 1) % 2, flat(c, P)], G["wp"][:, c, :],
                                      start=c == 0, stop=c == DC - 1)
                        last.then_inc(pr_done, 1)
                    if live(0):
                        pe.wait_ge(ax_in[s], slot(g, s, 0, 32))
                        after(pe, atT_ok, upto(g, s, 1))
                        for c in range(DC):
                            last = nc.tensor.transpose(at_ps[:, flat(c, P)], at[:, s, flat(c, P)], ident)
                        last.then_inc(at_done, 1)
                    if live(3):
                        pe.wait_ge(xhT_ok, upto(g, s, 3))
                        after(pe, lg_ok, upto(g, s, 4))
                        for c in range(DC):
                            last = mm(lg_ps[:, 0:E], xhT[:, (s - 3) % 2, flat(c, P)], G["rwT"][:, c, :],
                                      start=c == 0, stop=c == DC - 1)
                        last.then_inc(lg_done, 1)
                    if live(2):
                        pe.wait_ge(xh_ok, upto(g, s, 2))
                        after(pe, xhT_ok, upto(g, s, 3))
                        for c in range(DC):
                            last = nc.tensor.transpose(xh_ps[:, flat(c, P)], xh[:, (s - 2) % RING, flat(c, P)], ident)
                        last.then_inc(xh_done, 1)
                groups(pe, step)

            @block.scalar
            def _(act):
                def step(g, s, live):
                    if live(0):
                        act.wait_ge(at_done, upto(g, s, 0))
                        after(act, pr_done, upto(g, s, 2))
                        nc.scalar.activation(atT[:, s % 2, :], at_ps[:, 0:D], ACT.Copy).then_inc(atT_ok, 1)
                        act.wait_ge(w_in[s], slot(g, s, 0))
                        nc.scalar.activation(G["experts"][:, ds(g * (8 * HID) + s * 2 * HID, HID)], w[:, s, :],
                                             ACT.Copy, scale=WSCALE).then_inc(whi_ok, 1)
                    if live(2):
                        act.wait_ge(xh_done, upto(g, s, 2))
                        after(act, lg_done, upto(g, s, 4))
                        nc.scalar.activation(xhT[:, s % 2, :], xh_ps[:, 0:D], ACT.Copy).then_inc(xhT_ok, 1)
                groups(act, step)

            @block.vector
            def _(dve):
                def step(g, s, live):
                    if live(4):
                        dve.wait_ge(lg_done, upto(g, s, 4))
                        nc.vector.tensor_scalar(G["logits"][:, ds(g * RING + (s - 4), 1), :], lg_ps[:, None, 0:E],
                                                1.0, None, ALU.mult) \
                            .then_inc(lg_ok, 1)
                    if live(1):
                        k = (s - 1) % RING
                        hi = g * (8 * HID) + (s - 1) * 2 * HID
                        dve.wait_ge(whi_ok, upto(g, s, 1))
                        nc.vector.scalar_tensor_tensor(G["experts"][:, ds(hi + HID, HID)], w[:, k, :], WSCALE,
                                                       G["experts"][:, ds(hi, HID)], ALU.mult, ALU.subtract).then_inc(wlo_ok, 1)
                        dve.wait_ge(pr_done, upto(g, s, 1))
                        if not (isinstance(g, int) and g * RING + s < 5):
                            dve.wait_ge(x1_out[k], slot(g, s, 5, 32) + AHEAD)
                        nc.vector.tensor_tensor(x1[:, k, :], pr_ps[:, 0:D], x[:, k, :], ALU.add).then_inc(x1_ok, 1)
                        dve.wait_ge(x1_ok, upto(g, s, 1))
                        normed(nc, dve, x1[:, k, :], stats[:, k, :], mv[:, k, :], ve[:, k, :], ch, upto(g, s, 1, 2, 0), var_ok,
                               G["dve_passed"])
                        dve.wait_ge(rstd_ok, upto(g, s, 1))
                        nc.vector.tensor_scalar(xh[:, k, :], x1[:, k, :], mv[:, k, 0:1], rstd[:, k, :],
                                                ALU.subtract, ALU.mult).then_inc(xh_ok, 1)
                groups(dve, step)


def route(nc, A, G):
    Q = NT // 4
    with ExitStack() as ctx:
        L = Place(nc, ctx)
        te, et = [P, NT, E], [P, E, NT]
        mx, z, v1, v2, f1, f2, den = (L.sb(f"{n}_r", [P, NT]) for n in ("mx", "z", "v1", "v2", "f1", "f2", "den"))
        ex, pr, eq, pr2 = (L.sb(f"{n}_r", te) for n in ("ex", "pr", "eq", "pr2"))
        m1, m2 = L.sb("m1_r", te), L.sb("m2_r", te)
        both = L.sb("both_r", et, F16)
        tot, inc, pos, tmp = (L.sb(f"{n}_r", et) for n in ("tot", "inc", "pos", "tmp"))
        nb, ends, base = (L.sb(f"{n}_r", [P, E]) for n in ("nb", "ends", "base"))
        nbi = L.sb("nbi_r", [P, E], I32)
        ones = L.sb("ones_r", [P, E])
        slotf = L.sb("slotf_r", [P, NT, 2])
        sloti = L.sb("sloti_r", [P, NT, 2], I32)
        hi_i = L.sb("hi_i_r", [P, NT, 2], I32)
        hi_f, lo_f = L.sb("hi_f_r", [P, NT, 2]), L.sb("lo_f_r", [P, NT, 2])
        cmp_, cnt = L.sb("cmp_r", [1, ET, E]), L.sb("cnt_r", [1, ET])
        rowhot = L.sb("rowhot_r", [P, 2, Q, 2, P], F16)
        halfhot = L.sb("halfhot_r", [P, 2, Q, 2, HALFT], F16)
        tokhot = L.sb("tokhot_r", [P, 2, Q, 2, 2, HALFT], F16)
        tab = L.sb("tab_r", [P, HALFT])
        rank_ps, tot_ps, tab_ps = L.bank("rank_ps"), L.bank("tot_ps"), L.bank("tab_ps")
        ch, s_shift, s_exp, s_both, s_cnt, s_hot, s_place, s_tile, s_tab = (
            L.sem(f"{n}_r") for n in ("ch", "shift", "exp", "both", "cnt", "hot", "place", "tile", "tab"))
        col = lambda n: G["const"][:, CC[n][0]:CC[n][1]]
        with nc.Block() as block:

            @block.scalar
            def _(act):
                act.wait_ge(s_shift, 1)
                nc.scalar.activation(ex[:, :, :], pr2[:, :, :], ACT.Exp).then_inc(s_exp, 1)
                for q in range(4):
                    act.wait_ge(s_hot, 2 * q + 2)
                    after(act, s_tab, q - 1)
                    nc.scalar.activation(tokhot[:, q % 2, :, :, 1, :], halfhot[:, q % 2, :, :, :], ACT.Copy,
                                         scale=col("part")).then_inc(s_place, 1)

            @block.tensor
            def _(pe):
                mm = nc.tensor.matmul
                pe.wait_ge(s_both, 1)
                m = both[:, :, :].rearrange("p e t -> p (e t)")
                mm(rank_ps[:, 0:E * NT], G["tri16"][:, :], m, start=True, stop=True)
                mm(tot_ps[:, 0:E * NT], G["ones16"][:, :], m, start=True, stop=True).then_inc(s_cnt, 1)
                for q in range(4):
                    pe.wait_ge(s_place, q + 1)
                    pe.wait_ge(s_tile, q + 1)
                    for t in range(q * Q, (q + 1) * Q):
                        for c in range(2):
                            last = mm(tab_ps[:, 0:2 * HALFT], rowhot[:, q % 2, t % Q, c, :],
                                      tokhot[:, q % 2, t % Q, c, :, :].rearrange("p a h -> p (a h)"),
                                      start=t == 0 and c == 0, stop=t == NT - 1 and c == 1)
                    last.then_inc(s_tab, 1)

            @block.vector
            def _(dve):
                count = [0]

                def link(ins):
                    count[0] += 1
                    ins.then_inc(ch, 1)
                    dve.wait_ge(ch, count[0])

                v = nc.vector
                lg = G["logits"]
                wide = lambda a: a[:, :, None].broadcast_to(te)
                link(v.tensor_reduce(mx[:, :], lg[:, :, :], AX.X, ALU.max))
                v.tensor_tensor(pr2[:, :, :], lg[:, :, :], wide(mx), ALU.subtract).then_inc(s_shift, 1)
                dve.wait_ge(s_exp, 1)
                link(v.tensor_reduce(z[:, :], ex[:, :, :], AX.X, ALU.add))
                link(v.reciprocal(mx[:, :], z[:, :]))
                link(v.tensor_tensor(pr[:, :, :], ex[:, :, :], wide(mx), ALU.mult))
                rank8 = col("rank8")[:, None, :].broadcast_to(te)

                def largest(p, val, f, m):
                    link(v.tensor_reduce(val[:, :], p[:, :, :], AX.X, ALU.max))
                    link(v.tensor_tensor(eq[:, :, :], p[:, :, :], wide(val), ALU.is_equal))
                    link(v.tensor_tensor(eq[:, :, :], eq[:, :, :], rank8, ALU.mult))
                    link(v.tensor_reduce(f[:, :], eq[:, :, :], AX.X, ALU.max))
                    link(v.tensor_tensor(m[:, :, :], rank8, wide(f), ALU.is_equal))

                largest(pr, v1, f1, m1)
                link(v.scalar_tensor_tensor(pr2[:, :, :], m1[:, :, :], -2.0, pr[:, :, :], ALU.mult, ALU.add))
                largest(pr2, v2, f2, m2)
                v.tensor_tensor(both[:, :, :].rearrange("p e t -> p t e"), m1[:, :, :], m2[:, :, :], ALU.add).then_inc(s_both, 1)
                link(v.tensor_tensor(den[:, :], v1[:, :], v2[:, :], ALU.add))
                link(v.tensor_scalar(den[:, :], den[:, :], 1e-9, None, ALU.add))
                link(v.reciprocal(z[:, :], den[:, :]))
                for n, val in enumerate((v1, v2)):
                    v.tensor_tensor(G["cw_t"][:, :, n, :].rearrange("p s b -> p b s"),
                                    val[:, :].rearrange("p (b s) -> p b s", b=B),
                                    z[:, :].rearrange("p (b s) -> p b s", b=B), ALU.mult)
                v.memset(ones[:, :], 1.0)
                dve.wait_ge(s_cnt, 1)
                link(v.tensor_copy(tot[:, :, :], tot_ps[:, 0:E * NT].rearrange("p (e t) -> p e t", e=E)))
                fl = lambda a: a[:, :, :].rearrange("p e t -> p (e t)")
                link(v.tensor_tensor_scan(fl(inc), col("restart"), fl(tot), 0.0, ALU.mult, ALU.add))
                link(v.tensor_scalar(nb[:, :], inc[:, :, NT - 1], float(SLOTS - 1), None, ALU.add))
                link(v.tensor_copy(nbi[:, :], nb[:, :]))
                link(v.tensor_scalar(nbi[:, :], nbi[:, :], SLOTS.bit_length() - 1, None, ALU.arith_shift_right))
                link(v.tensor_copy(nb[:, :], nbi[:, :]))
                link(v.tensor_tensor_scan(ends[:, :], ones[:, :], nb[:, :], 0.0, ALU.mult, ALU.add))
                link(v.tensor_tensor(base[:, :], ends[:, :], nb[:, :], ALU.subtract))
                link(v.tensor_scalar(base[:, :], base[:, :], float(SLOTS), None, ALU.mult))
                link(v.tensor_tensor(pos[:, :, :], inc[:, :, :], tot[:, :, :], ALU.subtract))
                link(v.tensor_tensor(pos[:, :, :], pos[:, :, :],
                                     rank_ps[:, 0:E * NT].rearrange("p (e t) -> p e t", e=E), ALU.add))
                link(v.tensor_tensor(pos[:, :, :], pos[:, :, :], base[:, :, None].broadcast_to(et), ALU.add))
                for n, m in enumerate((m1, m2)):
                    link(v.tensor_tensor(tmp[:, :, :], pos[:, :, :], m[:, :, :].rearrange("p t e -> p e t"), ALU.mult))
                    link(v.tensor_reduce(slotf[:, :, n], tmp[:, :, :].rearrange("p e t -> p t e"), AX.X, ALU.add))
                link(v.tensor_copy(sloti[:, :, :], slotf[:, :, :]))
                v.tensor_copy(G["slots_t"][:, :, :, :], sloti[:, :, :].rearrange("p (b s) n -> p s n b", b=B))
                link(v.tensor_scalar(hi_i[:, :, :], sloti[:, :, :], 7, None, ALU.arith_shift_right))
                link(v.tensor_copy(hi_f[:, :, :], hi_i[:, :, :]))
                link(v.scalar_tensor_tensor(lo_f[:, :, :], hi_f[:, :, :], -float(P), slotf[:, :, :], ALU.mult, ALU.add))
                for q in range(4):
                    part = flat(q, Q)
                    after(dve, s_tab, q - 1)
                    after(dve, s_place, q - 1)
                    v.tensor_tensor(rowhot[:, q % 2, :, :, :].rearrange("p t c r -> p (t c) r"),
                                    col("rowid")[:, None, :].broadcast_to([P, 2 * Q, P]),
                                    lo_f[:, part, :].rearrange("p t c -> p (t c)")[:, :, None].broadcast_to([P, 2 * Q, P]),
                                    ALU.is_equal).then_inc(s_hot, 1)
                    v.tensor_tensor(halfhot[:, q % 2, :, :, :].rearrange("p t c r -> p (t c) r"),
                                    col("halfid")[:, None, :].broadcast_to([P, 2 * Q, HALFT]),
                                    hi_f[:, part, :].rearrange("p t c -> p (t c)")[:, :, None].broadcast_to([P, 2 * Q, HALFT]),
                                    ALU.is_equal).then_inc(s_hot, 1)
                    dve.wait_ge(s_hot, 2 * q + 2)
                    v.tensor_tensor(tokhot[:, q % 2, :, :, 0, :], halfhot[:, q % 2, :, :, :],
                                    col("tileid")[:, part, None, None].broadcast_to([P, Q, 2, HALFT]), ALU.mult).then_inc(s_tile, 1)
                link(v.tensor_scalar(ends[:, :], ends[:, :], float(SLOTS), None, ALU.mult))
                link(v.tensor_tensor(cmp_[:, :, :], col("slot0")[0:1, :, None].broadcast_to([1, ET, E]),
                                     ends[0:1, None, :].broadcast_to([1, ET, E]), ALU.is_ge))
                link(v.tensor_reduce(cnt[:, :], cmp_[:, :, :], AX.X, ALU.add))
                link(v.tensor_scalar(cnt[:, :], cnt[:, :], float(E - 1), None, ALU.min))
                v.tensor_copy(G["tile_expert"][:, :], cnt[:, :])
                dve.wait_ge(s_tab, 4)
                link(v.tensor_scalar(tab[:, :], tab_ps[:, 0:HALFT], float(P), None, ALU.mult))
                link(v.tensor_tensor(tab[:, :], tab[:, :], tab_ps[:, HALFT:2 * HALFT], ALU.add))
                v.tensor_copy(G["token"][:, :], tab[:, :])


def experts(nc, A, G):
    with ExitStack() as ctx:
        L = Place(nc, ctx)
        idx = L.sb("idx_e", [P, 2], I32)
        x = L.sb("x_e", [P, 2, D])
        xT = [L.sb(f"xT_e{i}", [P, DC, SLOTS], F16) for i in range(2)]
        h = L.sb("h_e", [P, 2, 2 * SLOTS])
        hh = [L.sb(f"hh_e{i}", [P, 2, 2 * SLOTS], F16) for i in range(2)]
        y = L.sb("y_e", [P, 2, D])
        xT_ps = L.bank("xT_ps_e")
        up_ps = [L.bank(f"up_ps{i}") for i in range(4)]
        y_ps = [L.bank(f"y_ps{i}") for i in range(2)]
        idx_ok, x_in, xT_done, xhi_ok, xlo_ok, up_done = (
            L.sem(f"{n}_e") for n in ("idx_ok", "x_in", "xT_done", "xhi_ok", "xlo_ok", "up_done"))
        gelu_ok, hhi_ok, hlo_ok, down_done, y_done, y_ok, y_out = (
            L.sem(f"{n}_e") for n in ("gelu_ok", "hhi_ok", "hlo_ok", "down_done", "y_done", "y_ok", "y_out"))
        ident = G["const"][:, CC["ident"][0]:CC["ident"][1]]
        QS = 4

        def tiles(eng, step):
            step(0, True)
            with eng.Fori(1, ET - 1) as k:
                step(k, True)
            step(ET - 1, False)

        with nc.Block() as block:

            @block.gpsimd
            def _(pool):
                def step(k, more):
                    after(pool, xT_done, k)
                    nc.gpsimd.tensor_copy(idx[:, :], G["token"][:, ds(k * 2, 2)]).then_inc(idx_ok, 1)
                    apart(pool, idx_ok, k + 1, G["pool_passed"])
                    for n in range(2):
                        pool.indirect_dma_start(out=x[:, n, :], out_offset=None, in_=A["xh"],
                                                in_offset=bass.IndirectOffsetOnAxis(ap=idx[:, n:n + 1], axis=0)) \
                            .then_inc(x_in, 16)
                tiles(pool, step)

            @block.sync
            def _(sp):
                def step(k, more):
                    sp.wait_ge(y_ok, 2 * k + 2)
                    sp.dma_start(A["y"][ds(k * SLOTS, SLOTS), :].rearrange("(n p) d -> p n d", p=P), y[:, :, :]) \
                        .then_inc(y_out, 16)
                tiles(sp, step)
                sp.wait_ge(y_out, 16 * ET)

            @block.tensor
            def _(pe):
                mm = nc.tensor.matmul

                def transpose(k):
                    pe.wait_ge(x_in, k * 32 + 32)
                    after(pe, xlo_ok, k)
                    for c in range(DC):
                        for n in range(2):
                            last = nc.tensor.transpose(xT_ps[:, ds(c * SLOTS + n * P, P)], x[:, n, flat(c, P)], ident)
                    last.then_inc(xT_done, 1)

                def step(k, more):
                    expert = pe.value_load(G["tile_expert"][0:1, ds(k, 1)], min_val=0, max_val=E - 1)
                    at = pe.snap(expert * (8 * HID))
                    W = G["experts"]

                    def up(q):
                        after(pe, gelu_ok, k * QS + q - 3)
                        for m in (2 * q, 2 * q + 1):
                            out = up_ps[q][:, flat(m % 2, SLOTS)]
                            for c in range(DC):
                                w = [W[:, ds(at + (c * 2 * HID + half * HID + m * P), P)] for half in range(2)]
                                mm(out, w[0], xT[0][:, c, :], start=c == 0, stop=False)
                                mm(out, w[0], xT[1][:, c, :], start=False, stop=False)
                                last = mm(out, w[1], xT[0][:, c, :], start=False, stop=c == DC - 1)
                        last.then_inc(up_done, 1)

                    def down(q):
                        pe.wait_ge(hlo_ok, k * QS + q + 1)
                        if q == 0:
                            after(pe, y_ok, 2 * k)
                        for m in (2 * q, 2 * q + 1):
                            w = [W[:, ds(at + ((2 + m // 4) * 2 * HID + half * HID + m % 4 * D), D)] for half in range(2)]
                            for n in range(2):
                                a = [hh[half][:, q % 2, ds(m % 2 * SLOTS + n * P, P)] for half in range(2)]
                                out = y_ps[n][:, 0:D]
                                mm(out, a[0], w[0], start=m == 0, stop=False)
                                mm(out, a[0], w[1], start=False, stop=False)
                                last = mm(out, a[1], w[0], start=False, stop=m == 7)
                        last.then_inc(down_done, 1)

                    pe.wait_ge(xlo_ok, k + 1)
                    up(0)
                    up(1)
                    up(2)
                    down(0)
                    up(3)
                    down(1)
                    if more:
                        transpose(k + 1)
                    down(2)
                    down(3)

                transpose(0)
                tiles(pe, step)

            @block.scalar
            def _(act):
                def rows(k):
                    act.wait_ge(xT_done, k + 1)
                    after(act, up_done, k * QS)
                    nc.scalar.activation(xT[0][:, :, :], xT_ps[:, :].rearrange("p (c t) -> p c t", c=DC), ACT.Copy) \
                        .then_inc(xhi_ok, 1)

                def step(k, more):
                    for q in range(QS):
                        act.wait_ge(up_done, k * QS + q + 1)
                        after(act, hlo_ok, k * QS + q - 1)
                        nc.scalar.activation(h[:, q % 2, :], up_ps[q][:, :], ACT.Gelu, scale=1 / WSCALE).then_inc(gelu_ok, 1)
                    if more:
                        rows(k + 1)
                    act.wait_ge(down_done, k * QS + QS)
                    after(act, y_out, k * 16)
                    for n in range(2):
                        nc.scalar.activation(y[:, n, :], y_ps[n][:, 0:D], ACT.Copy, scale=1 / WSCALE).then_inc(y_ok, 1)

                rows(0)
                tiles(act, step)

            @block.vector
            def _(dve):
                def rows(k):
                    dve.wait_ge(xhi_ok, k + 1)
                    nc.vector.tensor_tensor(xT[1][:, :, :], xT_ps[:, :].rearrange("p (c t) -> p c t", c=DC),
                                            xT[0][:, :, :], ALU.subtract).then_inc(xlo_ok, 1)

                def step(k, more):
                    for q in range(QS):
                        dve.wait_ge(gelu_ok, k * QS + q + 1)
                        after(dve, down_done, k * QS + q - 1)
                        nc.vector.tensor_copy(hh[0][:, q % 2, :], h[:, q % 2, :]).then_inc(hhi_ok, 1)
                        dve.wait_ge(hhi_ok, k * QS + q + 1)
                        nc.vector.tensor_tensor(hh[1][:, q % 2, :], h[:, q % 2, :], hh[0][:, q % 2, :], ALU.subtract) \
                            .then_inc(hlo_ok, 1)
                    if more:
                        rows(k + 1)

                rows(0)
                tiles(dve, step)


def feed_forward(nc, A, G):
    U = 4 * P
    with ExitStack() as ctx:
        L = Place(nc, ctx)
        at = L.sb("at_f", [P, 4, D])
        x2 = L.sb("x2_f", [P, 4, D])
        atT = L.sb("atT_f", [P, 2, D])
        x3 = L.sb("x3_f", [P, 8, D])
        xh = L.sb("xh_f", [P, 4, D])
        xhT = L.sb("xhT_f", [P, 2, DC, U])
        stats, mv = L.sb("stats_f", [P, 4, 6]), L.sb("mv_f", [P, 4, 2])
        ve, rstd = L.sb("ve_f", [P, 4, 1]), L.sb("rstd_f", [P, 4, 1])
        bo = L.sb("bo_f", [P, D])
        u1 = L.sb("u1_f", [P, DC, 2, RANK])
        w1 = L.sb("v1_f", [2 * RANK, HID])
        w1h = L.sb("v1h_f", [2 * RANK, HID], F16)
        b1 = L.sb("b1_f", [P, HID // P])
        u2 = L.sb("u2_f", [P, HID // P, RANK])
        w2 = L.sb("v2_f", [RANK + 1, D])
        lhi = L.sb("lhi_f", [2 * RANK, U], F16)
        llo = L.sb("llo_f", [RANK, U], F16)
        h = L.sb("h_f", [P, 2, U])
        low2 = L.sb("low2_f", [RANK + 1, U])
        out = L.sb("out_f", [P, 4, D])
        at_ps, pr_ps, xh_ps, low_ps, low2_ps, out_ps = (L.bank(f"{n}_ps_f") for n in ("at", "pr", "xh", "low", "low2", "out"))
        h_ps = [L.bank(f"h_ps{i}_f") for i in range(2)]
        outs_ps = [out_ps, h_ps[0]]
        w_in = L.sem("w_in_f")
        ax_in = [L.sem(f"ax_in{i}_f") for i in range(4)]
        res_out = L.sem("res_out")
        at_done, atT_ok, pr_done, x3a_ok, llo_ok, ch, var_ok, rstd_ok, xh_ok, xh_done, xhT_ok = (
            L.sem(f"{n}_f") for n in ("at_done", "atT_ok", "pr_done", "x3a_ok", "llo_ok", "ch", "var_ok", "rstd_ok", "xh_ok",
                                      "xh_done", "xhT_ok"))
        low_done, low_ok, h_done, h_ok, back_done, low2_ok, out_done, out_ok = (
            L.sem(f"{n}_f") for n in ("low_done", "low_ok", "h_done", "h_ok", "back_done", "low2_ok", "out_done", "out_ok"))
        ident = G["const"][:, CC["ident"][0]:CC["ident"][1]]
        MS = HID // P
        LOADS = 9

        AHEAD = 16

        def bodies(eng, step, ahead=False):
            def body(bb, lo, hi, end):
                for s in range(TB):
                    step(bb, s, lambda k: lo <= s - k < (hi if k >= 0 else end))
            body(0, 0, TB, TB + 1)
            with eng.Fori(1, B - 1 if ahead else B) as bb:
                body(bb, -TB, TB, TB + 1)
            if ahead:
                body(B - 1, -TB, TB, TB)
            body(B, -TB, 0, 0)

        def upto(bb, s, back, per=1, plus=1):
            return bb * (TB * per) + ((s - back) * per + plus)

        def slot(bb, s, back, per=16):
            return bb * (2 * per) + ((s - back) // 4 + 1) * per

        def phase(s):
            return (s + 2) % 4

        def unit(bb, s, per=1, plus=0):
            return bb * (2 * per) + ((s - 6 - phase(s)) // 4 * per + plus)

        SCHEDULE = {0: [("h", 0), ("h", 1), ("b", 0), ("h", 2), ("b", 1)],
                    1: [("h", 3), ("b", 2), ("h", 4), ("b", 3), ("h", 5), ("b", 4)],
                    2: [("h", 6), ("b", 5), ("h", 7), ("b", 6), ("b", 7)],
                    3: ["out"]}

        with nc.Block() as block:

            @block.sync
            def _(sp):
                sp.dma_start(bo[:, :], A["L1_xattn_bo"][None, :].broadcast_to([P, D])).then_inc(w_in, 16)
                for n in range(2):
                    sp.dma_start(u1[:, :, n, :], A["L1_ffn_U1"].rearrange("(c p) r -> p c r", p=P)).then_inc(w_in, 16)
                    sp.dma_start(w1[n * RANK:(n + 1) * RANK, :], A["L1_ffn_V1"]).then_inc(w_in, 16)
                with nc.allow_non_contiguous_dma(reason="a thousand biases, onto partitions"):
                    sp.dma_start(b1[:, :], A["L1_ffn_b1"].rearrange("(m p) -> p m", p=P)).then_inc(w_in, 16)
                sp.dma_start(u2[:, :, :], A["L1_ffn_U2"].rearrange("(m p) r -> p m r", p=P)).then_inc(w_in, 16)
                sp.dma_start(w2[0:RANK, :], A["L1_ffn_V2"]).then_inc(w_in, 16)
                sp.dma_start(w2[RANK:RANK + 1, :], A["L1_ffn_b2"][None, :]).then_inc(w_in, 16)

                sp.sem_inc(res_out, AHEAD)

                def load(bb, s):
                    row = ds(bb * S + s * P, P)
                    after(sp, x3a_ok, upto(bb, s, 4))
                    sp.dma_start(at[:, s % 4, :], A["attn1"][row, :]).then_inc(ax_in[s % 4], 16)
                    sp.dma_start(x2[:, s % 4, :], A["x2"][row, :]).then_inc(ax_in[s % 4], 16)

                load(0, 0)

                def step(bb, s, live):
                    if live(-1):
                        load(bb, s + 1)
                    if phase(s) == 0 and live(10):
                        row = ds(bb * S + (s - 10) * P, U)
                        sp.wait_ge(out_ok, unit(bb, s, 2, AHEAD))
                        sp.dma_start(A["out"].rearrange("b s d -> (b s) d")[row, :].rearrange("(i p) d -> p i d", p=P),
                                     out[:, :, :]).then_inc(res_out, 16)
                bodies(sp, step, ahead=True)
                sp.wait_ge(res_out, 16 * NT // 4 + AHEAD)

            @block.gpsimd
            def _(pool):
                def step(bb, s, live):
                    if live(1):
                        k = (s - 1) % 4
                        pool.wait_ge(var_ok, upto(bb, s, 1))
                        nc.gpsimd.tensor_tensor(rstd[:, k, :], ve[:, k, :], G["neghalf"][:, :], ALU.pow).then_inc(rstd_ok, 1)
                bodies(pool, step)

            @block.tensor
            def _(pe):
                mm = nc.tensor.matmul
                pe.wait_ge(w_in, 16 * LOADS)

                def step(bb, s, live):
                    if phase(s) == 0 and live(6):
                        par = (s - 6) % TB // 4
                        pe.wait_ge(xhT_ok, unit(bb, s, 4, 4))
                        pe.wait_ge(llo_ok, unit(bb, s, 1, 2))
                        for c in range(DC):
                            last = mm(low_ps[:, :], u1[:, c, :, :].rearrange("p n r -> p (n r)"), xhT[:, par, c, :],
                                      start=c == 0, stop=c == DC - 1)
                        last.then_inc(low_done, 1)
                    if live(1):
                        pe.wait_ge(atT_ok, upto(bb, s, 1))
                        after(pe, x3a_ok, upto(bb, s, 2))
                        for c in range(DC):
                            last = mm(pr_ps[:, 0:D], atT[:, (s - 1) % 2, flat(c, P)], G["woT"][:, c, :],
                                      start=c == 0, stop=c == DC - 1)
                        last.then_inc(pr_done, 1)
                    if live(0):
                        pe.wait_ge(ax_in[s % 4], slot(bb, s, 0, 32))
                        after(pe, atT_ok, upto(bb, s, 1))
                        for c in range(DC):
                            last = nc.tensor.transpose(at_ps[:, flat(c, P)], at[:, s % 4, flat(c, P)], ident)
                        last.then_inc(at_done, 1)
                    ph = phase(s)
                    if live(6 + ph):
                        par = (s - 6 - ph) % TB // 4
                        for item in SCHEDULE[ph]:
                            if item == "out":
                                pe.wait_ge(low2_ok, unit(bb, s, 1, 1))
                                pe.wait_ge(out_ok, unit(bb, s, 2, AHEAD))
                                for i in range(4):
                                    last = mm(outs_ps[i // 2][:, flat(i % 2, D)], low2[:, flat(i, P)], w2[:, :],
                                              start=True, stop=True)
                                    if i % 2:
                                        last.then_inc(out_done, 1)
                            elif item[0] == "h":
                                m = item[1]
                                if m == 0:
                                    pe.wait_ge(llo_ok, unit(bb, s, 1, 3))
                                    pe.wait_ge(out_ok, unit(bb, s, 2, AHEAD))
                                after(pe, h_ok, unit(bb, s, MS, m - 1))
                                mm(h_ps[m % 2][:, :], w1h[:, flat(m, P)], lhi[:, :], start=True, stop=False)
                                mm(h_ps[m % 2][:, :], w1h[0:RANK, flat(m, P)], llo[:, :], start=False, stop=True) \
                                    .then_inc(h_done, 1)
                            else:
                                m = item[1]
                                pe.wait_ge(h_ok, unit(bb, s, MS, m + 1))
                                if m == 0:
                                    after(pe, low2_ok, unit(bb, s))
                                mm(low2_ps[0:RANK, :], u2[:, m, :], h[:, m % 2, :], start=m == 0, stop=m == MS - 1) \
                                    .then_inc(back_done, 1)
                    if live(2):
                        pe.wait_ge(xh_ok, upto(bb, s, 2))
                        after(pe, xhT_ok, upto(bb, s, 3))
                        for c in range(DC):
                            last = nc.tensor.transpose(xh_ps[:, flat(c, P)], xh[:, (s - 2) % 4, flat(c, P)], ident)
                        last.then_inc(xh_done, 1)
                bodies(pe, step)

            @block.scalar
            def _(act):
                act.wait_ge(w_in, 16 * LOADS)

                def step(bb, s, live):
                    if phase(s) == 0 and live(6):
                        act.wait_ge(low_done, unit(bb, s, 1, 1))
                        after(act, h_done, unit(bb, s, MS))
                        nc.scalar.activation(lhi[:, :], low_ps[:, :], ACT.Copy).then_inc(low_ok, 1)
                    if live(0):
                        act.wait_ge(at_done, upto(bb, s, 0))
                        after(act, pr_done, upto(bb, s, 2))
                        nc.scalar.activation(atT[:, s % 2, :], at_ps[:, 0:D], ACT.Copy).then_inc(atT_ok, 1)
                    ph = phase(s)
                    if live(6 + ph):
                        for item in SCHEDULE[ph]:
                            if item[0] == "h":
                                m = item[1]
                                act.wait_ge(h_done, unit(bb, s, MS, m + 1))
                                after(act, back_done, unit(bb, s, MS, m - 1))
                                nc.scalar.activation(h[:, m % 2, :], h_ps[m % 2][:, :], ACT.Gelu_apprx_tanh,
                                                     bias=b1[:, m:m + 1], scale=1 / WSCALE).then_inc(h_ok, 1)
                    if live(2):
                        k = (s - 2) % TB
                        act.wait_ge(xh_done, upto(bb, s, 2))
                        if k % 4 == 0:
                            after(act, low_done, bb * 2 + ((s - 2) // 4 - 1))
                        nc.scalar.activation(xhT[:, k // 4, :, flat(k % 4, P)],
                                             xh_ps[:, 0:D].rearrange("p (c t) -> p c t", c=DC), ACT.Copy).then_inc(xhT_ok, 1)
                bodies(act, step)

            @block.vector
            def _(dve):
                nc.vector.memset(low2[RANK:RANK + 1, :], 1.0)
                dve.sem_inc(out_ok, AHEAD)
                dve.wait_ge(w_in, 16 * LOADS)
                nc.vector.tensor_scalar(w1h[:, :], w1[:, :], WSCALE, None, ALU.mult).then_inc(llo_ok, 1)
                dve.wait_ge(llo_ok, 1)
                nc.vector.scalar_tensor_tensor(w1h[RANK:2 * RANK, :], w1[RANK:2 * RANK, :], WSCALE, w1h[RANK:2 * RANK, :],
                                               ALU.mult, ALU.subtract).then_inc(llo_ok, 1)

                def step(bb, s, live):
                    ph = phase(s)
                    if ph == 0 and live(6):
                        dve.wait_ge(low_ok, unit(bb, s, 1, 1))
                        nc.vector.tensor_tensor(llo[:, :], low_ps[0:RANK, :], lhi[0:RANK, :], ALU.subtract).then_inc(llo_ok, 1)
                    if ph == 3 and live(9):
                        for i in range(2):
                            dve.wait_ge(out_done, unit(bb, s, 2, i + 1))
                            if i == 0:
                                dve.wait_ge(res_out, unit(bb, s, 16, AHEAD))
                            nc.vector.tensor_tensor(out[:, 2 * i:2 * i + 2, :], outs_ps[i][:, :].rearrange("p (i d) -> p i d", i=2),
                                                    x3[:, ds((s - 9) % TB + 2 * i, 2), :], ALU.add) \
                                .then_inc(out_ok, 1)
                    if live(1):
                        k = (s - 1) % 4
                        if ph == 3 and live(9):
                            dve.wait_ge(out_ok, unit(bb, s, 2, 2 + AHEAD))
                        dve.wait_ge(pr_done, upto(bb, s, 1))
                        nc.vector.tensor_tensor(x3[:, (s - 1) % TB, :], pr_ps[:, 0:D], x2[:, k, :], ALU.add).then_inc(x3a_ok, 1)
                        dve.wait_ge(x3a_ok, upto(bb, s, 1))
                        nc.vector.tensor_tensor(x3[:, (s - 1) % TB, :], x3[:, (s - 1) % TB, :], bo[:, :], ALU.add).then_inc(ch, 1)
                        dve.wait_ge(ch, upto(bb, s, 1, 3, 1))
                        normed(nc, dve, x3[:, (s - 1) % TB, :], stats[:, k, :], mv[:, k, :], ve[:, k, :], ch,
                               upto(bb, s, 1, 3, 1), var_ok, G["dve_passed"])
                        dve.wait_ge(rstd_ok, upto(bb, s, 1))
                        after(dve, xh_done, upto(bb, s, 5))
                        nc.vector.tensor_scalar(xh[:, k, :], x3[:, (s - 1) % TB, :], mv[:, k, 0:1], rstd[:, k, :],
                                                ALU.subtract, ALU.mult).then_inc(xh_ok, 1)
                    if ph == 2 and live(8):
                        dve.wait_ge(back_done, unit(bb, s, MS, MS))
                        after(dve, out_done, unit(bb, s, 2))
                        nc.vector.tensor_copy(low2[0:RANK, :], low2_ps[0:RANK, :]).then_inc(low2_ok, 1)
                bodies(dve, step)


def program(nc, A):
    for name, shape in (("values0", [B, KEYS * D]), ("attn", [B * S, D]), ("x1", [B * S, D]), ("xh", [B * S, D]),
                        ("y", [ET * SLOTS, D]), ("x2", [B * S, D]), ("attn1", [B * S, D])):
        A[name] = nc.dram_tensor(name + "_scratch", shape, F32).ap()
    with ExitStack() as ctx:
        G = allocate(nc, ctx)
        with ExitStack() as inner:
            allocate_first(nc, inner, G)
            prepare(nc, A, G)
            attention(nc, A, G, 0)
        with ExitStack() as inner:
            G["experts"] = Place(nc, inner).sb("experts", [P, E * 8 * HID], F16)
            project(nc, A, G)
            route(nc, A, G)
            experts(nc, A, G)
        attention(nc, A, G, 1)
        feed_forward(nc, A, G)


_INS = ["x", "ctx_1024", "L0_xattn_Wq", "L0_xattn_Wk", "L0_xattn_Wv", "L0_xattn_Wp", "L0_ffn_router_w", "L0_ffn_w1",
        "L0_ffn_w2", "L1_xattn_Wv", "L1_xattn_Wk", "L1_xattn_Wq", "L1_xattn_Wo", "L1_xattn_bo", "L1_ffn_U1", "L1_ffn_V1",
        "L1_ffn_b1", "L1_ffn_U2", "L1_ffn_V2", "L1_ffn_b2"]


def kernel(**inputs):
    import concourse.bacc as bacc
    from concourse.bass_utils import run_bass_kernel_spmd as run

    nc = bacc.Bacc("TRN2", target_bir_lowering=False, num_devices=1)
    arrays, args = {}, {}
    for name in _INS + ["const"]:
        a = np.ascontiguousarray(constants() if name == "const" else inputs[name])
        arrays[f"in_{name}"] = a
        args[name] = nc.dram_tensor(f"in_{name}", a.shape, mybir.dt.from_np(a.dtype), kind="ExternalInput").ap()
    args["out"] = nc.dram_tensor("out_0", (B, S, D), F32, kind="ExternalOutput").ap()
    program(nc, args)
    r = run(nc, [arrays], core_ids=[0])
    return r.results[0]["out_0"]
```
